# Optimizing a Trainium2 kernel written in Bass

```python
import numpy as np
import jax
import jax.numpy as jnp

def _softmax(x, axis=-1):
    return jax.nn.softmax(x, axis=axis)

def _gelu(x):
    return jax.nn.gelu(x, approximate=True)

def _silu(x):
    return jax.nn.silu(x)

def _sigmoid(x):
    return jax.nn.sigmoid(x)

def _layernorm(x, axis=-1, eps=1e-05):
    m = jnp.mean(x, axis=axis, keepdims=True)
    v = jnp.var(x, axis=axis, keepdims=True)
    return (x - m) / jnp.sqrt(v + eps)

def _scatter_add(tgt, idx, src, axis=0):
    return tgt.at[idx].add(src)

def _segment_sum(src, seg, n):
    return jax.ops.segment_sum(src, seg, n)
kernel_name = 'mk_xattn_ffn_d1_seqx_r2_017a25'

def setup_inputs(seed: int=0):
    np.random.seed(seed)
    _w = jnp.asarray

    def _rec_inputs():
        import jax
        import jax.numpy as jnp
        _rk = jax.random.key(seed)
        x = -0.0002928 + 1 * jax.random.normal(jax.random.fold_in(_rk, 1), (16, 512, 512), jnp.float32)
        _lenS = 512 - jax.random.randint(jax.random.fold_in(_rk, 7), (16,), 0, max(1, 512 // 4) + 1, jnp.int32)
        _lenS2 = 512 - jax.random.randint(jax.random.fold_in(_rk, 8), (16,), 0, max(1, 512 // 4) + 1, jnp.int32)
        _ctx_1024P = jax.random.normal(jax.random.fold_in(_rk, 11), (16, 16, 512), jnp.float32)
        _ctx_1024c = jax.random.dirichlet(jax.random.fold_in(_rk, 511), 0.3 * jnp.ones((16,), jnp.float32), (16, 512))
        _ctx_1024t = jnp.einsum('bsk,bkd->bsd', _ctx_1024c, _ctx_1024P)
        _ctx_1024t = _ctx_1024t * jax.lax.rsqrt(jnp.mean(jnp.square(_ctx_1024t)) + 1e-12) * 0.953939
        ctx_1024 = -1.39393e-06 + 0.999914 * (_ctx_1024t + 0.3 * jax.random.normal(jax.random.fold_in(_rk, 611), (16, 512, 512), jnp.float32))
        return (x, ctx_1024)
    x, ctx_1024 = _rec_inputs()

    def _L0_xattn_setup():
        import jax, jax.numpy as jnp
        import numpy as np
        EMBED_PHI = 512
        EMBED_F = 512
        HIDDEN_F = 512
        N_HEADS = 16
        B, S = (2, 1024)
        key = jax.random.key(seed)
        ks = jax.random.split(key, 9)
        sphi = 1.0 / np.sqrt(EMBED_PHI)
        sf = 1.0 / np.sqrt(EMBED_F)
        sh = 1.0 / np.sqrt(HIDDEN_F)
        return {'q': jax.random.normal(ks[0], (B, S, EMBED_PHI), jnp.float32), 'k': jax.random.normal(ks[1], (B, S, EMBED_PHI), jnp.float32), 'v': jax.random.normal(ks[2], (B, S, EMBED_F), jnp.float32), 'Wq': jax.random.normal(ks[3], (HIDDEN_F, EMBED_PHI), jnp.float32) * sphi, 'Wk': jax.random.normal(ks[4], (HIDDEN_F, EMBED_PHI), jnp.float32) * sphi, 'Wv': jax.random.normal(ks[5], (HIDDEN_F, EMBED_F), jnp.float32) * sf, 'bv': jax.random.normal(ks[6], (HIDDEN_F,), jnp.float32) * sf, 'Wo': jax.random.normal(ks[7], (EMBED_F, HIDDEN_F), jnp.float32) * sh, 'bo': jax.random.normal(ks[8], (EMBED_F,), jnp.float32) * sh}
    _L0_xattn_all = _L0_xattn_setup()
    _L0_xattn_in = {k: v for k, v in _L0_xattn_all.items() if k in ('Wq', 'Wk', 'Wv', 'bv', 'Wo', 'bo')}
    del _L0_xattn_all

    def _L0_ffn_setup():
        import jax, jax.numpy as jnp
        import numpy as np

        def _bitlinear(x, w_latent):
            scale = jax.lax.stop_gradient(jnp.clip(jnp.mean(jnp.abs(w_latent), axis=1, keepdims=True), 1e-05, None))
            tern = jnp.clip(jnp.round(w_latent / scale), -1.0, 1.0)
            w = w_latent + jax.lax.stop_gradient(tern - w_latent)
            return x @ (w * scale).T
        key = jax.random.key(seed)
        ks = jax.random.split(key, 6)
        dim, hidden, rank = (512, 2048, 16)
        B, S = (4, 2048)
        x = jax.random.normal(ks[0], (B, S, dim), dtype=jnp.float32)
        w_fc = 0.02 * jax.random.normal(ks[1], (hidden, dim), dtype=jnp.float32)
        w_proj = 0.02 * jax.random.normal(ks[2], (dim, hidden), dtype=jnp.float32)
        u = 0.02 * jax.random.normal(ks[3], (hidden, rank), dtype=jnp.float32)
        v = 0.02 * jax.random.normal(ks[4], (rank, dim), dtype=jnp.float32)
        fast_b = jax.random.normal(ks[5], (rank, rank), dtype=jnp.float32)
        gate = jnp.float32(0.05)
        return {'x': x, 'fast_b': fast_b, 'w_fc': w_fc, 'w_proj': w_proj, 'u': u, 'v': v, 'gate': gate}
    _L0_ffn_all = _L0_ffn_setup()
    _L0_ffn_in = {k: v for k, v in _L0_ffn_all.items() if k in ('fast_b', 'w_fc', 'w_proj', 'u', 'v', 'gate')}
    del _L0_ffn_all
    return {'x': x, 'ctx_1024': ctx_1024, 'L0_xattn_Wq': _L0_xattn_in['Wq'], 'L0_xattn_Wk': _L0_xattn_in['Wk'], 'L0_xattn_Wv': _L0_xattn_in['Wv'], 'L0_xattn_bv': _L0_xattn_in['bv'], 'L0_xattn_Wo': _L0_xattn_in['Wo'], 'L0_xattn_bo': _L0_xattn_in['bo'], 'L0_ffn_fast_b': _L0_ffn_in['fast_b'], 'L0_ffn_w_fc': _L0_ffn_in['w_fc'], 'L0_ffn_w_proj': _L0_ffn_in['w_proj'], 'L0_ffn_u': _L0_ffn_in['u'], 'L0_ffn_v': _L0_ffn_in['v'], 'L0_ffn_gate': _L0_ffn_in['gate']}

def reference(x, ctx_1024, L0_xattn_Wq, L0_xattn_Wk, L0_xattn_Wv, L0_xattn_bv, L0_xattn_Wo, L0_xattn_bo, L0_ffn_fast_b, L0_ffn_w_fc, L0_ffn_w_proj, L0_ffn_u, L0_ffn_v, L0_ffn_gate):
    import jax
    import jax.numpy as jnp

    def _L0_xattn_ref(q, k, v, Wq, Wk, Wv, bv, Wo, bo):
        import jax, jax.numpy as jnp
        import numpy as np
        EMBED_PHI = 512
        EMBED_F = 512
        HIDDEN_F = 512
        N_HEADS = 16
        B, S = (2, 1024)
        Bq, Sq, _ = q.shape
        hd = HIDDEN_F // N_HEADS
        scale = 1.0 / np.sqrt(hd)
        qh = (q @ Wq.T).reshape(Bq, Sq, N_HEADS, hd).transpose(0, 2, 1, 3)
        kh = (k @ Wk.T).reshape(Bq, Sq, N_HEADS, hd).transpose(0, 2, 1, 3)
        vh = (v @ Wv.T + bv).reshape(Bq, Sq, N_HEADS, hd).transpose(0, 2, 1, 3)
        scores = jnp.einsum('bhsd,bhtd->bhst', qh, kh) * scale
        mask = jnp.triu(jnp.ones((Sq, Sq), dtype=bool), k=0).at[0, 0].set(False)
        scores = jnp.where(mask, -jnp.inf, scores)
        probs = jax.nn.softmax(scores, axis=-1)
        out = jnp.einsum('bhst,bhtd->bhsd', probs, vh)
        out = out.transpose(0, 2, 1, 3).reshape(Bq, Sq, HIDDEN_F)
        return out @ Wo.T + bo

    def _L0_ffn_ref(x, fast_b, w_fc, w_proj, u, v, gate):
        import jax, jax.numpy as jnp
        import numpy as np

        def _bitlinear(x, w_latent):
            scale = jax.lax.stop_gradient(jnp.clip(jnp.mean(jnp.abs(w_latent), axis=1, keepdims=True), 1e-05, None))
            tern = jnp.clip(jnp.round(w_latent / scale), -1.0, 1.0)
            w = w_latent + jax.lax.stop_gradient(tern - w_latent)
            return x @ (w * scale).T
        h = _bitlinear(x, w_fc) + gate * (x @ v.T @ fast_b.T @ u.T)
        r = jnp.maximum(h, 0.0)
        return _bitlinear(r * r, w_proj)
    x = x + _L0_xattn_ref(_layernorm(x, axis=-1), ctx_1024, ctx_1024, L0_xattn_Wq, L0_xattn_Wk, L0_xattn_Wv, L0_xattn_bv, L0_xattn_Wo, L0_xattn_bo)
    x = x + _L0_ffn_ref(_layernorm(x, axis=-1), L0_ffn_fast_b, L0_ffn_w_fc, L0_ffn_w_proj, L0_ffn_u, L0_ffn_v, L0_ffn_gate)
    return x

_drawn_inputs = setup_inputs


def setup_inputs(seed=0):
    import zlib

    import numpy as np

    out = dict(_drawn_inputs(seed))
    spreads = {}
    factors = {'L0_ffn_fast_b': 8.0, 'L0_ffn_u': 8.0, 'L0_ffn_v': 8.0}
    for name, (base, spread) in spreads.items():
        noise = np.random.default_rng([zlib.crc32(name.encode()), seed]).standard_normal(out[name].shape)
        drawn = base * np.exp(spread * noise) if base else spread * noise
        out[name] = jnp.asarray(drawn.astype(out[name].dtype))
    for name, factor in factors.items():
        out[name] = (out[name] * factor).astype(out[name].dtype)
    return out
```

```python
from contextlib import ExitStack

import concourse.bass as bass
from concourse import mybir

F32 = mybir.dt.float32
F32R = mybir.dt.float32r
BF16 = mybir.dt.bfloat16
ALU = mybir.AluOpType
ACT = mybir.ActivationFunctionType
AX = mybir.AxisListType

P = 128
HEADS = 16
GROUPS = 4
GH = HEADS // GROUPS
EPS = 1e-5
MASKED = -1e30
UNITS = 10


MM_STEPS = ("W", "BIAS", "XT", "CT", "Q", "K", "V", "M", "OA")


def interleave(units, others):
    out = []
    for k, u in enumerate(units):
        out.append(u)
        out += others.get(k, [])
    return out


def setup_steps():
    return ([("W", w, k) for w in range(4) for k in range(4)] + [("BIAS",)]
            + [("LN_STATS",), ("LN_APPLY",)] + [("XT", k) for k in range(4)] + [("CT", k) for k in range(4)]
            + [("Q", 0), ("K", 0)])


def batch_steps(more):
    def nxt(*steps):
        return list(steps) if more else []

    def st(g):
        return [x for k in range(UNITS) for x in ((("S", g + 1, k),) + (("T", g, k),))]

    steps = [("XRES",)]
    steps += interleave([("S", 0, k) for k in range(UNITS)],
                        {1: [("V", 0)], 3: [("Q", 1)], 4: [("K", 1)], 5: [("V", 1)], 7: [("V", 2)]})
    steps += [("M", 0), ("V", 3), ("Q", 2), ("K", 2)]
    steps += interleave(st(0), {5: nxt(("LN_STATS",)), 13: nxt(("LN_APPLY",))})
    steps += [("M", 1), ("PV", 0)]
    steps += interleave(st(1), {1: [("Q", 3)], 5: [("K", 3)], 9: [("NORM", 0)]})
    steps += [("M", 2), ("PV", 1)]
    steps += interleave(st(2), {2: [("NORM", 1)], 5: nxt(("XT", 0)), 9: nxt(("XT", 1)), 13: nxt(("XT", 2)),
                                17: nxt(("XT", 3))})
    steps += [("M", 3), ("PV", 2)]
    steps += interleave([("T", 3, k) for k in range(UNITS)],
                        {0: [("NORM", 2)], 1: nxt(("Q", 0)), 3: [("OA", 0)], 5: [("OA", 1)], 7: [("OA2", 2)],
                         9: [("OA2", 3)]})
    steps += [("PV", 3), ("NORM", 3)] + [("OC", j) for j in range(4)] + [("OB", j) for j in range(4)]
    steps += nxt(*[("CT", k) for k in range(4)], ("K", 0))
    return steps


def is_next(step, in_batch):
    return in_batch and (step[0] in ("LN_STATS", "LN_APPLY", "XT", "CT") or step[:2] in (("Q", 0), ("K", 0)))


def count_mm(steps):
    return sum(s[0] in MM_STEPS for s in steps)


def wait_alone(engine, passed, *waits):
    for sem, value in waits:
        engine.wait_ge(sem, value)
        engine.sem_inc(passed, 1)


class Tally:

    def __init__(self, sem, base=0):
        self.sem, self.base, self.local = sem, base, 0

    def inc(self, instruction):
        instruction.then_inc(self.sem, 1)
        self.local += 1

    def now(self):
        return self.base + self.local


def layernorm_buffers(sb, tt):
    shapes = {"stats": [P, tt, 6], "mean_var": [P, tt, 2], "v": [P, tt], "log": [P, tt], "y": [P, tt], "t": [P, tt],
              "rstd": [P, tt]}
    return {name: sb(f"ln_{name}", shape) for name, shape in shapes.items()}


def ln_stats(dve, chain, ln, rows, passed):
    tt = rows.shape[1]
    for j in range(tt):
        chain.inc(dve.bn_stats(ln["stats"][:, j, :], rows[:, j, :]))
    wait_alone(dve, passed, (chain.sem, chain.now()))
    for j in range(tt):
        chain.inc(dve.bn_aggr(ln["mean_var"][:, j, :], ln["stats"][:, j, :]))
    dve.wait_ge(chain.sem, chain.now())
    return dve.tensor_scalar(ln["v"][:, :], ln["mean_var"][:, :, 1], EPS, None, ALU.add)


def ln_rstd(act, chain, ln):
    chain.inc(act.activation(ln["log"][:, :], ln["v"][:, :], ACT.Ln))
    act.wait_ge(chain.sem, chain.now())
    return act.activation(ln["y"][:, :], ln["log"][:, :], ACT.Exp, scale=-0.5)


def ln_apply(dve, chain, ln, rows, x_hat, ready):
    t, y, v, rstd = (ln[k][:, :] for k in ("t", "y", "v", "rstd"))
    for step in (lambda: dve.tensor_tensor(t, y, y, ALU.mult), lambda: dve.tensor_tensor(t, t, v, ALU.mult),
                 lambda: dve.tensor_scalar(t, t, -0.5, 1.5, ALU.mult, ALU.add),
                 lambda: dve.tensor_tensor(rstd, y, t, ALU.mult)):
        chain.inc(step())
        dve.wait_ge(chain.sem, chain.now())
    for j in range(rows.shape[1]):
        dve.tensor_scalar(x_hat[:, j, :], rows[:, j, :], ln["mean_var"][:, j, 0:1], ln["rstd"][:, j:j + 1],
                          ALU.subtract, ALU.mult).then_inc(ready, 1)


def attention_phase(nc, dram, batches):
    x, ctx_in, Wq, Wk, Wv, bv, Wo, bo, x2_out = dram
    S, D = x.shape[1], x.shape[2]
    KT = D // P
    TT = S // P
    HD = D // HEADS
    SCALE = float(HD) ** -0.5
    assert (S, D, HD, KT, TT) == (512, 512, 32, 4, 4)

    SETUP, STEADY, LAST = setup_steps(), batch_steps(True), batch_steps(False)
    MM0, MMB = count_mm(SETUP), count_mm(STEADY)
    assert MMB % 2 == 0
    SB = UNITS * GROUPS + 2
    TB = UNITS * GROUPS

    with ExitStack() as c:
        def sb(name, shape, dt=F32):
            return c.enter_context(nc.sbuf_tensor(name, shape, dt))

        def sem(name):
            return c.enter_context(nc.semaphore(name))

        wT_hi = sb("wT_hi", [P, 4, KT, D], F32R)
        wT_lo = sb("wT_lo", [P, 4, KT, D], F32R)
        stack = [sb(f"stack{s}", [P, 2, GH, S], F32R) for s in range(2)]
        stage = sb("stage", [P, 4, S], F32R)
        probs = sb("probs", [P, UNITS, S])
        xT_hi = sb("xT_hi", [P, KT, S], F32R)
        xT_lo = sb("xT_lo", [P, KT, S], F32R)
        cT_hi = sb("cT_hi", [P, KT, S], F32R)
        cT_lo = sb("cT_lo", [P, KT, S], F32R)
        v_sb = sb("v_sb", [P, TT, D])
        x_in = sb("x_in", [P, TT, D])
        x_res = sb("x_res", [P, TT, D])
        c_in = sb("c_in", [P, TT, D])
        x_hat = sb("x_hat", [P, TT, D])
        o_recip = sb("o_recip", [P, S])
        o_norm = sb("o_norm", [P, S])
        bias_sb = sb("bias_sb", [P, D])
        ident = sb("ident", [P, P])
        ident_bf = sb("ident_bf", [P, P], BF16)
        masks = sb("masks", [P, 2, P], BF16)
        ones = sb("ones", [P, P])
        maxima = sb("maxima", [P, P])
        m_stage = sb("m_stage", [16, 2, P], F32R)
        bv_col = sb("bv_col", [P, GROUPS])
        ln = layernorm_buffers(sb, TT)

        bank = [c.enter_context(nc.psum_tensor(f"bank{n}", [P, 512], F32)) for n in range(8)]
        mm_bank, s_bank, t_bank, o_bank, sum_bank = bank[0:2], bank[2:4], bank[4:6], bank[6], bank[7]

        w_loaded = [sem(f"w_loaded{n}") for n in range(4)]
        b_loaded = sem("b_loaded")
        x_loaded = sem("x_loaded")
        c_loaded = sem("c_loaded")
        consts_ready = sem("consts_ready")
        mm_full = sem("mm_full")
        mm_hi = sem("mm_hi")
        mm_free = sem("mm_free")
        s_full = sem("s_full")
        s_free = sem("s_free")
        t_full = sem("t_full")
        exp_done = sem("exp_done")
        selected = sem("selected")
        pv_done = sem("pv_done")
        o_normed = sem("o_normed")
        ot_hi = sem("ot_hi")
        ot_ready = sem("ot_ready")
        qk_stacked = [[sem(f"qk_stacked{s}{p}") for p in range(2)] for s in range(2)]
        m_stacked = [sem(f"m_stacked{s}") for s in range(2)]
        var_ready = sem("var_ready")
        rstd_ready = sem("rstd_ready")
        act_self = sem("act_self")
        dve_self = sem("dve_self")
        xhat_ready = sem("xhat_ready")
        xres_ready = sem("xres_ready")
        x2_stored = sem("x2_stored")
        sp_passed, pool_passed, dve_passed = sem("sp_passed"), sem("pool_passed"), sem("dve_passed")

        CONSTS = 11
        MM_BIAS = 17
        HI_SKIP = sum(s[0] in ("V", "OA") for s in STEADY)
        CHAIN0, CHAIN = 12, 16

        block = c.enter_context(nc.Block())

        STACKED = (slice(0, 3, 2), slice(1, 3, 1), slice(0, 4, 3))
        QS, KS = 0, 1

        def jobs(steps, first, parity):
            n = 0
            for s in steps:
                if s[0] in MM_STEPS:
                    yield s, first + n, mm_bank[(parity + n) % 2]
                    n += 1
                else:
                    yield s, None, None

        def in_loop(engine, program):
            program(SETUP, None, 0, 0)
            if batches > 1:
                with engine.Fori(0, batches - 1, 1) as i:
                    program(STEADY, i, i * MMB + MM0, MM0 % 2)
            program(LAST, batches - 1, (batches - 1) * MMB + MM0, MM0 % 2)

        def batch_of(step, i):
            return 0 if i is None else i + 1 if is_next(step, True) else i

        def staged(eng, sems, g, b, each):
            if g > 0:
                eng.wait_ge(sems[(g - 1) % 2], (b * 2 + (g - 1) // 2 + 1) * each)
            elif not isinstance(b, int) or b > 0:
                eng.wait_ge(sems[1], b * 2 * each)

        @block.sync
        def _(sp):
            def stack_qk(g, b, pair):
                for h in (2 * pair, 2 * pair + 1):
                    for r, pick in enumerate(STACKED):
                        sp.dma_start(stack[g % 2][32 * r:32 * r + 32, :, h, :].bitcast(F32),
                                     stage[32 * h:32 * h + 32, pick, :].bitcast(F32)
                                     ).then_inc(qk_stacked[g % 2][pair], 16)

            def program(steps, i, first, parity):
                if i is None:
                    for w, (dst, src) in enumerate(((x_in, Wq), (c_in, Wk), (x_hat, Wv), (x_res, Wo))):
                        sp.dma_start(dst[:, :, :], src.rearrange("(j p) d -> p j d", p=P)).then_inc(w_loaded[w], 16)
                    with nc.allow_non_contiguous_dma(reason="512 values, once"):
                        sp.dma_start(bv_col[:, :], bv.rearrange("(g p) -> p g", p=P)).then_inc(b_loaded, 16)
                    sp.dma_start(o_recip[0:1, :], bo.rearrange("(a d) -> a d", a=1)).then_inc(b_loaded, 16)
                pending = None
                for s, n, _ in jobs(steps, first, parity):
                    b = batch_of(s, i)
                    if s == ("W", 1, 0) and i is None:
                        sp.wait_ge(mm_full, 4)
                        sp.dma_start(x_in[:, :, :], x[0].rearrange("(j p) d -> p j d", p=P)).then_inc(x_loaded, 16)
                    elif s == ("W", 2, 0) and i is None:
                        sp.wait_ge(mm_full, 8)
                        sp.dma_start(c_in[:, :, :], ctx_in[0].rearrange("(j p) d -> p j d", p=P)
                                     ).then_inc(c_loaded, 16)
                    elif s[0] == "XRES" and steps is STEADY:
                        wait_alone(sp, sp_passed, (mm_free, first))
                        sp.dma_start(c_in[:, :, :], ctx_in[bass.ds(i + 1, 1)].rearrange("a (j p) d -> p (a j) d", p=P)
                                     ).then_inc(c_loaded, 16)
                        wait_alone(sp, sp_passed, (xres_ready, i * TT + TT))
                        sp.dma_start(x_in[:, :, :], x[bass.ds(i + 1, 1)].rearrange("a (j p) d -> p (a j) d", p=P)
                                     ).then_inc(x_loaded, 16)
                    elif s[0] == "K" and s[1] < 2:
                        g = s[1]
                        wait_alone(sp, sp_passed, (mm_free, n + 1))
                        stack_qk(g, b, 0)
                        stack_qk(g, b, 1)
                    elif s[0] == "T" and s[1] < 2 and s[2] == 4:
                        g = s[1] + 2
                        if s[1] == 0:
                            wait_alone(sp, sp_passed, (mm_free, k_job[2] + 1))
                        else:
                            wait_alone(sp, sp_passed, (mm_free, k_job[3] + 1))
                        wait_alone(sp, sp_passed, (t_full, i * TB + UNITS * s[1] + 5))
                        stack_qk(g, b, 0)
                        pending = g
                    elif s[0] == "M":
                        g = s[1]
                        wait_alone(sp, sp_passed, (mm_free, n + 1))
                        for part in range(2):
                            sp.dma_start(stack[g % 2][96 + part:97 + part, QS, :, :].bitcast(F32)
                                         .rearrange("p h (r s) -> p (h r) s", s=P),
                                         m_stage[:, part, :].bitcast(F32)).then_inc(m_stacked[g % 2], 16)
                        if pending is not None:
                            wait_alone(sp, sp_passed, (t_full, i * TB + UNITS * (pending - 2) + UNITS))
                            stack_qk(pending, b, 1)
                            pending = None
                    elif s[0] == "OB":
                        wait_alone(sp, sp_passed, (s_free, i * SB + TB + s[1] - 1) if s[1] >= 2
                                   else (mm_free, oa_job[s[1]] + 1))
                        sp.dma_start(x2_out[bass.ds(i * TT + s[1], 1)].rearrange("a p d -> p (a d)"),
                                     x_res[:, s[1], :]).then_inc(x2_stored, 16)
                    if s[0] == "K":
                        k_job[s[1]] = n
                    if s[0] == "OA":
                        oa_job[s[1]] = n
                if steps is LAST:
                    sp.wait_ge(x2_stored, 16 * TT * batches)

            k_job, oa_job = {}, {}
            in_loop(sp, program)

        @block.gpsimd
        def _(pool):
            consts = Tally(consts_ready)
            consts.inc(pool.memset(ident[:, :], 0.0))
            consts.inc(pool.memset(ident_bf[:, :], 0.0))
            consts.inc(pool.memset(masks[:, :, :], 0.0))
            consts.inc(pool.memset(ones[:, :], 1.0))
            consts.inc(pool.memset(maxima[:, :], 0.0))
            pool.wait_ge(consts_ready, consts.now())
            for m in (ident, ident_bf):
                consts.inc(pool.affine_select(out=m[:, :], in_=m[:, :], compare_op=ALU.not_equal, fill=1.0,
                                              base=0, pattern=[[-1, P]], channel_multiplier=1))
            consts.inc(pool.affine_select(out=masks[:, 0, :], in_=masks[:, 0, :], compare_op=ALU.is_ge, fill=MASKED,
                                          base=0, pattern=[[-(P + 1), P]], channel_multiplier=P))
            consts.inc(pool.affine_select(out=masks[:, 1, :], in_=masks[:, 1, :], compare_op=ALU.is_ge, fill=MASKED,
                                          base=-1, pattern=[[-1, P]], channel_multiplier=1))
            for s in range(2):
                pool.wait_ge(consts_ready, consts.now())
                consts.inc(pool.memset(stack[s][96:98, KS, :, :].bitcast(F32), -1.0))
            pool.wait_ge(consts_ready, CONSTS)

            def select(view, count, first_block):
                return pool.affine_select(out=view, in_=view, compare_op=ALU.is_ge, fill=0.0,
                                          base=0 if first_block else -1,
                                          pattern=[[0, count], [P if first_block else 1, P]],
                                          channel_multiplier=-(P + 1) if first_block else -1)

            def program(steps, i, first, parity):
                for s, n, _ in jobs(steps, first, parity):
                    if s[0] == "XRES":
                        pool.wait_ge(x_loaded, i * 16 + 16)
                        pool.wait_ge(mm_free, first)
                        pool.wait_ge(x2_stored, i * 16 * TT)
                        for j in range(TT):
                            pool.tensor_tensor(x_res[:, j, :], x_in[:, j, :], bias_sb[:, :], ALU.add
                                               ).then_inc(xres_ready, 1)
                    elif s[0] == "T" and s[2] in (4, 9):
                        u = s[2] - 4
                        wait_alone(pool, pool_passed, (exp_done, i * TB + UNITS * s[1] + s[2] + 1))
                        blocks = probs[:, u:u + 5, :].rearrange("p u (c x) -> p u c x", x=P)
                        select(blocks[:, 0:4:2, 0, :], 2, True)
                        select(blocks[:, 1:2, 0:4:3, :].rearrange("p u c x -> p (u c) x"), 2, False)
                        select(blocks[:, 3:4, 0:4:3, :].rearrange("p u c x -> p (u c) x"), 2, False)
                        select(blocks[:, 4, 0:4:2, :], 2, False).then_inc(selected, 1)

            in_loop(pool, program)

        @block.tensor
        def _(pe):
            def split_product(out, a_hi, a_lo, b_hi, b_lo, tiles):
                pairs = [(a, b, k) for k in tiles for a, b in ((a_hi, b_hi), (a_hi, b_lo), (a_lo, b_hi))]
                for m, (a, b, k) in enumerate(pairs):
                    last = pe.matmul(out, a(k), b(k), start=m == 0, stop=m == len(pairs) - 1)
                return last

            def s_unit(g, k, out):
                st = stack[g % 2]
                pair, u = divmod(k, 5)

                def block(h, r, t1, cols):
                    pe.matmul(out[:, cols:cols + t1], st[0:96, QS, h, P * r:P * r + P], st[0:96, KS, h, 0:t1],
                              start=True, stop=False)
                    return pe.matmul(out[:, cols + t1 - P:cols + t1], ident_bf[:, :], masks[:, min(r, 1), :],
                                     start=False, stop=True)

                if u < 4 and u % 2 == 0:
                    return block(2 * pair + u // 2, 3, 512, 0)
                if u < 4:
                    block(2 * pair + u // 2, 2, 384, 0)
                    return block(2 * pair + u // 2, 0, 128, 384)
                block(2 * pair, 1, 256, 0)
                return block(2 * pair + 1, 1, 256, 256)

            def t_unit(g, k, out):
                st = stack[g % 2]
                pair, u = divmod(k, 5)

                def block(h, r, cols):
                    return pe.matmul(out[:, cols:cols + S - P * r], st[0:98, KS, h, P * r:P * r + P],
                                     st[0:98, QS, h, P * r:S], start=True, stop=True)

                if u < 4 and u % 2 == 0:
                    return block(2 * pair + u // 2, 0, 0)
                if u < 4:
                    block(2 * pair + u // 2, 1, 0)
                    return block(2 * pair + u // 2, 3, 384)
                block(2 * pair, 2, 0)
                return block(2 * pair + 1, 2, 256)

            def pv(g):
                for r in (0, 1, 3, 2):
                    for target in (o_bank, sum_bank):
                        for h in range(GH):
                            base = 5 * (h // 2)
                            unit, cols = {0: (base + 2 * (h % 2), 0), 1: (base + 2 * (h % 2) + 1, 0),
                                          3: (base + 2 * (h % 2) + 1, 384), 2: (base + 4, 256 * (h % 2))}[r]
                            weights = (v_sb[:, r, (GH * g + h) * HD:(GH * g + h + 1) * HD] if target is o_bank
                                       else ones[:, 0:HD])
                            last = pe.matmul(target[HD * h:HD * h + HD, P * r:S], weights,
                                             probs[:, unit, cols:cols + S - P * r], start=r == 0, stop=r == 2)
                return last

            def out_part(target, j, groups):
                pairs = [(a, b, g) for g in groups for a, b in ((cT_hi, wT_hi), (cT_hi, wT_lo), (cT_lo, wT_hi))]
                for m, (a, b, g) in enumerate(pairs):
                    last = pe.matmul(target[:, :], a[:, g, P * j:P * j + P], b[:, 3, g, :],
                                     start=g == 0 and m == 0, stop=g == GROUPS - 1 and m == len(pairs) - 1)
                return last

            def program(steps, i, first, parity):
                out_bank = {2: s_bank[0], 3: s_bank[1]}
                for s, n, out in jobs(steps, first, parity):
                    b = batch_of(s, i)
                    if n is not None and not (isinstance(n, int) and n < 2):
                        pe.wait_ge(mm_free, n - 1)
                    if s[0] == "W":
                        if s[2] == 0:
                            pe.wait_ge(w_loaded[s[1]], 16)
                            pe.wait_ge(consts_ready, CONSTS)
                        src = (x_in, c_in, x_hat, x_res)[s[1]]
                        for j in range(4):
                            last = pe.transpose(out[:, P * j:P * j + P], src[:, j, P * s[2]:P * s[2] + P], ident[:, :])
                        last.then_inc(mm_full, 1)
                    elif s[0] == "BIAS":
                        pe.wait_ge(ot_ready, 1)
                        split_product(out[:, :], lambda k: stage[:, 0, P * k:P * k + P],
                                      lambda k: stage[:, 1, P * k:P * k + P],
                                      lambda k: wT_hi[:, 3, k, :], lambda k: wT_lo[:, 3, k, :], range(4))
                        pe.matmul(out[:, :], ones[0:1, :], o_recip[0:1, :], start=False, stop=True,
                                  skip_group_check=True).then_inc(mm_full, 1)
                    elif s[0] in ("XT", "CT"):
                        if s[1] == 0:
                            if s[0] == "XT":
                                pe.wait_ge(xhat_ready, b * TT + TT)
                            else:
                                pe.wait_ge(c_loaded, b * 16 + 16)
                        src = x_hat if s[0] == "XT" else c_in
                        for j in range(TT):
                            last = pe.transpose(out[:, P * j:P * j + P], src[:, j, P * s[1]:P * s[1] + P], ident[:, :])
                        last.then_inc(mm_full, 1)
                    elif s[0] in ("Q", "K"):
                        w, t_hi, t_lo = (0, xT_hi, xT_lo) if s[0] == "Q" else (1, cT_hi, cT_lo)
                        if s[1] == 0:
                            pe.wait_ge(mm_free, transposed[s[0]] + 1)
                        g = s[1]
                        split_product(out[:, :], lambda k: wT_hi[:, w, k, P * g:P * g + P],
                                      lambda k: wT_lo[:, w, k, P * g:P * g + P],
                                      lambda k: t_hi[:, k, :], lambda k: t_lo[:, k, :], range(KT)
                                      ).then_inc(mm_full, 1)
                    elif s[0] == "V":
                        j = s[1]
                        split_product(out[:, :], lambda k: cT_hi[:, k, P * j:P * j + P],
                                      lambda k: cT_lo[:, k, P * j:P * j + P],
                                      lambda k: wT_hi[:, 2, k, :], lambda k: wT_lo[:, 2, k, :], range(KT)
                                      ).then_inc(mm_full, 1)
                        v_job = n
                    elif s[0] == "S":
                        u = UNITS * s[1] + s[2]
                        if s[2] in (0, 5):
                            pe.wait_ge(qk_stacked[s[1] % 2][s[2] // 5], (i * 2 + s[1] // 2 + 1) * 96)
                        pe.wait_ge(s_free, i * SB + max(u - 1, 0))
                        s_unit(s[1], s[2], s_bank[u % 2]).then_inc(s_full, 1)
                    elif s[0] == "M":
                        pe.wait_ge(s_free, i * SB + UNITS * s[1] + UNITS)
                        pe.transpose(out[:, 0:P], maxima[:, :], ident[:, :]).then_inc(mm_full, 1)
                    elif s[0] == "T":
                        u = UNITS * s[1] + s[2]
                        if s[2] == 0:
                            pe.wait_ge(m_stacked[s[1] % 2], (i * 2 + s[1] // 2 + 1) * 32)
                        if u >= 2:
                            pe.wait_ge(exp_done, i * TB + u - 1)
                        t_unit(s[1], s[2], t_bank[u % 2]).then_inc(t_full, 1)
                    elif s[0] == "PV":
                        if s[1] == 0:
                            pe.wait_ge(mm_free, v_job + 1)
                        pe.wait_ge(selected, i * 8 + 2 * s[1] + 2)
                        pe.wait_ge(o_normed, i * GROUPS + s[1] + 1)
                        pv(s[1]).then_inc(pv_done, 1)
                    elif s[0] in ("OA", "OA2"):
                        if s[0] == "OA":
                            out_bank[s[1]] = out
                        else:
                            pe.wait_ge(s_free, i * SB + TB)
                        if s[1] == 0:
                            pe.wait_ge(ot_ready, i * GROUPS + 3)
                        out_part(out_bank[s[1]], s[1], (0, 1))
                    elif s[0] == "OC":
                        if s[1] == 0:
                            pe.wait_ge(ot_ready, i * GROUPS + 4)
                        out_part(out_bank[s[1]], s[1], (2,))
                    elif s[0] == "OB":
                        if s[1] == 0:
                            pe.wait_ge(ot_ready, i * GROUPS + 5)
                        out_part(out_bank[s[1]], s[1], (3,)).then_inc(mm_full if s[1] < 2 else s_full, 1)
                    if s[0] in ("XT", "CT"):
                        transposed["Q" if s[0] == "XT" else "K"] = n

            transposed = {}
            in_loop(pe, program)

        @block.scalar
        def _(act):
            def program(steps, i, first, parity):
                chain = Tally(act_self, 0 if i is None else i + 1)
                for s, n, out in jobs(steps, first, parity):
                    b = batch_of(s, i)
                    if s[0] in ("W", "XT", "CT", "Q", "K", "M"):
                        act.wait_ge(mm_full, n + 1)
                        if s[0] == "W":
                            dst = wT_hi[:, s[1], s[2], :]
                        elif s[0] == "XT":
                            dst = xT_hi[:, s[1], :]
                        elif s[0] == "CT":
                            dst = cT_hi[:, s[1], :]
                        elif s[0] == "M":
                            staged(act, m_stacked, s[1], b, 32)
                            act.activation(m_stage[:, 0, :], out[0:16, 0:P], ACT.Copy).then_inc(mm_hi, 1)
                            continue
                        else:
                            dst = stage[:, 0 if s[0] == "Q" else 2, :]
                            for p in range(2):
                                staged(act, [q[p] for q in qk_stacked], s[1], b, 96)
                            if s == ("Q", 0) and i is None:
                                act.wait_ge(mm_full, MM_BIAS)
                        act.activation(dst, out[:, :], ACT.Copy).then_inc(mm_hi, 1)
                    elif s[0] == "BIAS":
                        act.wait_ge(o_normed, 1)
                        act.activation(stage[:, 0, :], o_norm[:, :], ACT.Copy).then_inc(ot_hi, 1)
                        act.wait_ge(mm_full, n + 1)
                        act.activation(bias_sb[:, :], out[:, :], ACT.Copy).then_inc(mm_hi, 1)
                    elif s[0] in ("V", "OA"):
                        pass
                    elif s[0] == "LN_STATS":
                        act.wait_ge(var_ready, b + 1)
                        ln_rstd(act, chain, ln).then_inc(rstd_ready, 1)
                    elif s[0] == "T":
                        u = UNITS * s[1] + s[2]
                        act.wait_ge(t_full, i * TB + u + 1)
                        act.activation(probs[:, s[2], :], t_bank[u % 2][:, :], ACT.Exp, scale=SCALE
                                       ).then_inc(exp_done, 1)
                    elif s[0] == "NORM":
                        act.wait_ge(o_normed, i * GROUPS + s[1] + 2)
                        act.activation(cT_hi[:, s[1], :], o_norm[:, :], ACT.Copy).then_inc(ot_hi, 1)

            in_loop(act, program)

        @block.vector
        def _(dve):
            def program(steps, i, first, parity):
                chain = Tally(dve_self, 0 if i is None else i * CHAIN + CHAIN0)
                hi = 0 if i is None else i * (MMB - HI_SKIP) + MM0
                highs = 0
                for s, n, out in jobs(steps, first, parity):
                    b = batch_of(s, i)
                    if s[0] in ("W", "XT", "CT", "Q", "K", "M"):
                        rows, cols = (16, P) if s[0] == "M" else (P, 512)
                        a_hi, a_lo = {"W": lambda: (wT_hi[:, s[1], s[2], :], wT_lo[:, s[1], s[2], :]),
                                  "XT": lambda: (xT_hi[:, s[1], :], xT_lo[:, s[1], :]),
                                  "CT": lambda: (cT_hi[:, s[1], :], cT_lo[:, s[1], :]),
                                  "Q": lambda: (stage[:, 0, :], stage[:, 1, :]),
                                  "K": lambda: (stage[:, 2, :], stage[:, 3, :]),
                                  "M": lambda: (m_stage[:, 0, :], m_stage[:, 1, :])}[s[0]]()
                        highs += 1
                        dve.wait_ge(mm_hi, hi + highs)
                        dve.tensor_tensor(a_lo, out[0:rows, 0:cols], a_hi.bitcast(F32), ALU.subtract
                                          ).then_inc(mm_free, 1)
                    elif s[0] == "BIAS":
                        dve.wait_ge(b_loaded, 32)
                        dve.wait_ge(consts_ready, CONSTS)
                        for g in range(GROUPS):
                            last = dve.tensor_scalar(o_norm[:, P * g:P * g + P], ones[:, :], bv_col[:, g:g + 1], None,
                                                     ALU.mult)
                        last.then_inc(o_normed, 1)
                        dve.wait_ge(ot_hi, 1)
                        dve.tensor_tensor(stage[:, 1, :], o_norm[:, :], stage[:, 0, :].bitcast(F32), ALU.subtract
                                          ).then_inc(ot_ready, 1)
                        highs += 1
                        dve.wait_ge(mm_hi, hi + highs)
                        dve.tensor_copy(o_norm[:, :], bias_sb[:, :]).then_inc(mm_free, 1)
                    elif s[0] == "V":
                        dve.wait_ge(mm_full, n + 1)
                        dve.tensor_copy(v_sb[:, s[1], :], out[:, :]).then_inc(mm_free, 1)
                    elif s[0] == "S":
                        u = UNITS * s[1] + s[2]
                        bank_u = s_bank[u % 2]
                        pair, k = divmod(s[2], 5)
                        dve.wait_ge(s_full, i * SB + u + 1)
                        if k < 4 and k % 2 == 0:
                            col = 4 * (2 * pair + k // 2)
                            last = dve.tensor_reduce(maxima[:, col + 3:col + 4], bank_u[:, :], AX.X, ALU.max)
                        elif k < 4:
                            col = 4 * (2 * pair + k // 2)
                            dve.tensor_reduce(maxima[:, col + 2:col + 3], bank_u[:, 0:384], AX.X, ALU.max)
                            last = dve.tensor_reduce(maxima[:, col:col + 1], bank_u[:, 384:512], AX.X, ALU.max)
                        else:
                            col = 8 * pair + 1
                            last = dve.tensor_reduce(maxima[:, col:col + 5:4],
                                                     bank_u[:, :].rearrange("p (h t) -> p h t", h=2), AX.X, ALU.max)
                        last.then_inc(s_free, 1)
                    elif s[0] == "LN_STATS":
                        dve.wait_ge(x_loaded, b * 16 + 16)
                        ln_stats(dve, chain, ln, x_in, dve_passed).then_inc(var_ready, 1)
                    elif s[0] == "LN_APPLY":
                        dve.wait_ge(rstd_ready, b + 1)
                        ln_apply(dve, chain, ln, x_in, x_hat, xhat_ready)
                    elif s[0] == "NORM":
                        dve.wait_ge(pv_done, i * GROUPS + s[1] + 1)
                        chain.inc(dve.reciprocal(o_recip[:, :], sum_bank[:, :]))
                        dve.wait_ge(dve_self, chain.now())
                        dve.tensor_tensor(o_norm[:, :], o_bank[:, :], o_recip[:, :], ALU.mult).then_inc(o_normed, 1)
                        dve.wait_ge(ot_hi, i * GROUPS + s[1] + 2)
                        dve.tensor_tensor(cT_lo[:, s[1], :], o_norm[:, :], cT_hi[:, s[1], :].bitcast(F32), ALU.subtract
                                          ).then_inc(ot_ready, 1)
                    elif s[0] == "OA":
                        oa[s[1]] = (n, out)
                    elif s[0] == "OB":
                        j = s[1]
                        if j < 2:
                            dve.wait_ge(mm_full, oa[j][0] + 1)
                        else:
                            dve.wait_ge(s_full, i * SB + TB + j - 1)
                        if j == 0:
                            dve.wait_ge(xres_ready, i * TT + TT)
                        src = oa[j][1] if j < 2 else s_bank[j - 2]
                        dve.tensor_tensor(x_res[:, j, :], src[:, :], x_res[:, j, :], ALU.add
                                          ).then_inc(mm_free if j < 2 else s_free, 1)
                if steps is SETUP:
                    assert chain.local == CHAIN0
                elif steps is STEADY:
                    assert chain.local == CHAIN

            oa = {}
            in_loop(dve, program)




HIDDEN_LAG = 4


def ffn_steps(blocks, more):
    steps = [("COPY",)]
    for b in range(blocks):
        steps.append(("H", b))
        if b >= HIDDEN_LAG:
            steps.append(("Y", b - HIDDEN_LAG))
        if more and b == 5:
            steps.append(("LN_STATS",))
        if more and b == 7:
            steps.append(("LN_APPLY",))
    for m, b in enumerate(range(blocks - HIDDEN_LAG, blocks)):
        if more:
            steps.append(("XT", m))
        steps.append(("Y", b))
    steps += [("RES", j) for j in range(4)]
    if more:
        steps.insert(len(steps) - 4, ("Z",))
    return steps


def ffn_phase(nc, dram, batches):
    x2_in, fast_b, w_fc, w_proj, u_in, v_in, gate, y_out = dram
    HIDDEN, D = w_fc.shape
    RANK = u_in.shape[1]
    KT, NB, TT, OT = D // P, HIDDEN // P, 4, D // P
    S = TT * P
    CHUNKS = HIDDEN // D
    assert RANK <= 32 and D == 512 and KT == 4 and HIDDEN_LAG == KT
    STEADY, LAST = ffn_steps(NB, True), ffn_steps(NB, False)
    XJ = KT + 1
    RING = 8

    with ExitStack() as c:
        def sb(name, shape, dt=F32):
            return c.enter_context(nc.sbuf_tensor(name, shape, dt))

        def sem(name):
            return c.enter_context(nc.semaphore(name))

        fcT = sb("fcT", [P, KT, HIDDEN], F32R)
        projT = sb("projT", [P, NB, D], F32R)
        a_stack = sb("a_stack", [P, KT, P], F32R)
        u_stack = sb("u_stack", [P, HIDDEN], F32R)
        w_nat = sb("w_nat", [P, 4, D])
        tern = sb("tern", [P, 2, D], BF16)
        neg = sb("neg", [P, 2, D], BF16)
        u_nat = sb("u_nat", [P, NB, RANK])
        u_hi = sb("u_hi", [P, NB, RANK], F32R)
        u_lo = sb("u_lo", [P, NB, RANK], F32R)
        u_cols = sb("u_cols", [P, NB, P])
        v_sb = sb("v_rows", [RANK, D])
        fb_sb = sb("fb_sb", [RANK, RANK])
        fbT = sb("fbT", [RANK, RANK])
        gate_sb = sb("gate_sb", [1, 1])
        gate_col = sb("gate_col", [P, 1])
        a_f32 = sb("a_f32", [P, KT, RANK])
        scale_fc = sb("scale_fc", [P, NB])
        scale_pr = sb("scale_pr", [P, OT])
        parts = sb("parts", [P, NB + OT * CHUNKS])
        half = sb("half", [P, NB + OT])
        neg_half = sb("neg_half", [P, NB + OT])
        inv_fc = sb("inv_fc", [P, NB])
        diag = sb("diag", [P, OT, P])
        scale_row = sb("scale_row", [P, D])
        junk = sb("junk", [P, D])
        ident = sb("ident2", [P, P])
        ident_bf = sb("ident2_bf", [P, P], BF16)
        ones = sb("ones2", [P, P])
        xT_hi = sb("x2T_hi", [P, KT, S], F32R)
        xT_lo = sb("x2T_lo", [P, KT, S], F32R)
        x_in = sb("x2_in_sb", [P, TT, D])
        x_res = sb("x2_res", [P, TT, D])
        x_hat = sb("x2_hat", [P, TT, D])
        y_sb = sb("y_sb", [P, TT, D])
        z_sb = sb("z_sb", [P, S], F32R)
        relu = sb("relu", [P, 2, S])
        act_sq = sb("act_sq", [P, 2, S])
        a_hi = sb("a_hi", [P, RING, S], F32R)
        a_lo = sb("a_lo", [P, RING, S], F32R)
        ln = layernorm_buffers(lambda n, s: sb(f"{n}2", s), TT)

        h_bank = [c.enter_context(nc.psum_tensor(f"h_bank{n}", [P, 512], F32)) for n in range(2)]
        x_bank = [c.enter_context(nc.psum_tensor(f"x_bank{n}", [P, 512], F32)) for n in range(2)]
        y_bank = [c.enter_context(nc.psum_tensor(f"y_bank{n}", [P, 512], F32)) for n in range(4)]

        wn_loaded = [sem(f"wn_loaded{n}") for n in range(4)]
        small_loaded = sem("small_loaded")
        consts_ready = sem("consts2_ready")
        sums_ready = sem("sums_ready")
        tern_ready = sem("tern_ready")
        tern_full = sem("tern_full")
        tern_out = sem("tern_out")
        prep = sem("prep")
        x2_loaded = sem("x2_loaded")
        h_full = sem("h_full")
        relu_done = sem("relu_done")
        sq_done = sem("sq_done")
        hid_hi = sem("hid_hi")
        hid_ready = sem("hid_ready")
        y_full = sem("y_full")
        y_free = sem("y_free")
        y_ready = sem("y_ready")
        y_stored = sem("y_stored")
        xm_full = sem("xm_full")
        xm_hi = sem("xm_hi")
        xm_free = sem("xm_free")
        var_ready = sem("var2_ready")
        rstd_ready = sem("rstd2_ready")
        act_self = sem("act2_self")
        dve_self = sem("dve2_self")
        xhat_ready = sem("xhat2_ready")
        xres_ready = sem("xres2_ready")
        sp_passed, pool_passed, dve_passed = sem("sp2_passed"), sem("pool2_passed"), sem("dve2_passed")

        LOADS = [("fc", t, 0) for t in range(NB)] + [("pr", t, q) for t in range(OT) for q in range(CHUNKS)]
        CONSTS = 7
        CHAIN0 = CHAIN = 12

        block = c.enter_context(nc.Block())

        def in_loop(engine, program):
            if batches > 1:
                with engine.Fori(0, batches - 1, 1) as i:
                    program(STEADY, i)
            program(LAST, batches - 1)

        def row_loads(q):
            kind, t, _ = LOADS[q]
            return q + 1 if kind == "fc" else NB + (t + 1) * CHUNKS

        @block.sync
        def _(sp):
            nc_ctx = nc.allow_non_contiguous_dma(reason="rows of 16 values, once")
            with nc_ctx:
                sp.dma_start(u_nat[:, :, :], u_in.rearrange("(b p) r -> p b r", p=P)).then_inc(small_loaded, 16)
                sp.dma_start(v_sb[:, :], v_in).then_inc(small_loaded, 16)
                sp.dma_start(fb_sb[:, :], fast_b).then_inc(small_loaded, 16)
                sp.dma_start(gate_sb[:, :], gate).then_inc(small_loaded, 16)
            for q, (kind, t, piece) in enumerate(LOADS):
                if q >= 4:
                    sp.wait_ge(tern_ready, q - 3)
                rows = w_fc if kind == "fc" else w_proj
                sp.dma_start(w_nat[:, q % 4, :], rows[P * t:P * t + P, D * piece:D * piece + D]
                             ).then_inc(wn_loaded[q % 4], 16)
            sp.dma_start(x_in[:, :, :], x2_in[0:TT].rearrange("j p d -> p j d")).then_inc(x2_loaded, 16)

            def program(steps, i):
                for s in steps:
                    if s[0] == "COPY" and steps is STEADY:
                        wait_alone(sp, sp_passed, (xres_ready, i * TT + TT))
                        wait_alone(sp, sp_passed, (xm_free, i * XJ + XJ))
                        sp.dma_start(x_in[:, :, :], x2_in[bass.ds(i * TT + TT, TT)].rearrange("j p d -> p j d")
                                     ).then_inc(x2_loaded, 16)
                    elif s[0] == "RES":
                        wait_alone(sp, sp_passed, (y_ready, i * TT + s[1] + 1))
                        sp.dma_start(y_out[bass.ds(i * TT + s[1], 1)].rearrange("a p d -> p (a d)"), y_sb[:, s[1], :]
                                     ).then_inc(y_stored, 16)

            in_loop(sp, program)
            sp.wait_ge(y_stored, 16 * TT * batches)

        @block.gpsimd
        def _(pool):
            consts = Tally(consts_ready)
            consts.inc(pool.memset(ident[:, :], 0.0))
            consts.inc(pool.memset(ident_bf[:, :], 0.0))
            consts.inc(pool.memset(ones[:, :], 1.0))
            consts.inc(pool.memset(u_cols[:, :, :], 0.0))
            consts.inc(pool.memset(a_stack[:, :, :].bitcast(F32), 0.0))
            pool.wait_ge(consts_ready, consts.now())
            for m in (ident, ident_bf):
                consts.inc(pool.affine_select(out=m[:, :], in_=m[:, :], compare_op=ALU.not_equal, fill=1.0,
                                              base=0, pattern=[[-1, P]], channel_multiplier=1))

            def program(steps, i):
                for s in steps:
                    if s[0] == "COPY":
                        wait_alone(pool, pool_passed, (x2_loaded, i * 16 + 16), (y_ready, i * TT))
                        for j in range(TT):
                            pool.tensor_copy(x_res[:, j, :], x_in[:, j, :]).then_inc(xres_ready, 1)

            in_loop(pool, program)

        @block.tensor
        def _(pe):
            def transposed(target, src, k):
                for j in range(TT):
                    last = pe.transpose(target[:, P * j:P * j + P], src[:, j, P * k:P * k + P], ident[:, :])
                return last

            pe.wait_ge(consts_ready, CONSTS)
            for q in range(len(LOADS)):
                pe.wait_ge(tern_ready, q + 1)
                if q >= 2:
                    pe.wait_ge(tern_out, q - 1)
                out = h_bank[q % 2][:, 0:256].bitcast(BF16)
                for k in range(4):
                    last = pe.transpose(out[:, P * k:P * k + P], tern[:, q % 2, P * k:P * k + P], ident_bf[:, :])
                last.then_inc(tern_full, 1)
            pe.wait_ge(small_loaded, 64)
            pe.matmul(x_bank[0][0:RANK, 0:RANK], fb_sb[:, :], ident[0:RANK, 0:RANK], start=True, stop=True)
            pe.matmul(x_bank[0][:, 32:33], ones[0:1, :], gate_sb[:, :], start=True, stop=True).then_inc(prep, 1)
            pe.wait_ge(prep, 2)
            for k in range(KT):
                last = pe.matmul(x_bank[1][:, RANK * k:RANK * k + RANK], v_sb[:, P * k:P * k + P], fbT[:, :],
                                 start=True, stop=True)
            last.then_inc(prep, 1)
            pe.wait_ge(prep, 6)
            for b in range(NB):
                last = pe.transpose(y_bank[b // 4][:, P * (b % 4):P * (b % 4) + P], u_cols[:, b, :], ident[:, :])
            for j in range(OT):
                last = pe.matmul(x_bank[0][:, P * j:P * j + P], ones[:, :], diag[:, j, :], start=True, stop=True)
            last.then_inc(prep, 1)
            pe.wait_ge(prep, 8)
            pe.wait_ge(tern_out, len(LOADS))

            def z_product(n):
                pe.wait_ge(xm_free, n)
                for k in range(KT):
                    for part in (xT_hi, xT_lo):
                        last = pe.matmul(x_bank[0][:, :], a_stack[:, k, :], part[:, k, :],
                                         start=k == 0 and part is xT_hi, stop=k == KT - 1 and part is xT_lo)
                last.then_inc(xm_full, 1)

            pe.wait_ge(xhat_ready, TT)
            for k in range(KT):
                if k >= 2:
                    pe.wait_ge(xm_free, k - 1)
                transposed(x_bank[k % 2], x_hat, k).then_inc(xm_full, 1)
            z_product(KT)

            def program(steps, i):
                for s in steps:
                    if s[0] == "H":
                        b = s[1]
                        if b >= 2:
                            pe.wait_ge(relu_done, i * NB + b - 1)
                        else:
                            pe.wait_ge(relu_done, i * NB)
                        cols = slice(P * b, P * b + P)
                        for k in range(KT):
                            pe.matmul(h_bank[b % 2][:, :], fcT[:, k, cols], xT_hi[:, k, :], start=k == 0, stop=False)
                            pe.matmul(h_bank[b % 2][:, :], fcT[:, k, cols], xT_lo[:, k, :], start=False, stop=False)
                        if b == 0:
                            pe.wait_ge(xm_free, i * XJ + XJ)
                        pe.matmul(h_bank[b % 2][:, :], u_stack[:, cols], z_sb[:, :], start=False, stop=True
                                  ).then_inc(h_full, 1)
                    elif s[0] == "Y":
                        b = s[1]
                        pe.wait_ge(hid_ready, i * NB + b + 1)
                        if b == 0:
                            pe.wait_ge(y_free, i * TT)
                        for j in range(TT):
                            pe.matmul(y_bank[j][:, :], a_hi[:, b % RING, P * j:P * j + P], projT[:, b, :],
                                      start=b == 0, stop=False)
                            last = pe.matmul(y_bank[j][:, :], a_lo[:, b % RING, P * j:P * j + P], projT[:, b, :],
                                             start=False, stop=b == NB - 1)
                        last.then_inc(y_full, 1)
                    elif s[0] == "XT":
                        k = s[1]
                        n = i * XJ + XJ + k
                        if k == 0:
                            pe.wait_ge(xhat_ready, i * TT + 2 * TT)
                        pe.wait_ge(xm_free, n if k == 0 else n - 1)
                        transposed(x_bank[k % 2], x_hat, k).then_inc(xm_full, 1)
                    elif s[0] == "Z":
                        z_product(i * XJ + XJ + KT)

            in_loop(pe, program)

        @block.scalar
        def _(act):
            def row_sum(q):
                act.wait_ge(wn_loaded[q % 4], q // 4 * 16 + 16)
                act.activation(junk[:, :], w_nat[:, q % 4, :], ACT.Abs, accum_out=parts[:, q:q + 1]
                               ).then_inc(sums_ready, 1)
                act.wait_ge(sums_ready, q + 1)

            def tern_copy(q):
                kind, t, piece = LOADS[q]
                act.wait_ge(tern_full, q + 1)
                src = h_bank[q % 2][:, 0:256].bitcast(BF16).rearrange("p (k c) -> p k c", k=4)
                dst = fcT[:, :, P * t:P * t + P] if kind == "fc" else projT[:, 4 * piece:4 * piece + 4,
                                                                          P * t:P * t + P]
                act.activation(dst, src, ACT.Copy).then_inc(tern_out, 1)

            copied = 0
            for q in range(len(LOADS)):
                row_sum(q)
                while copied < len(LOADS) and row_loads(copied) <= q - 1:
                    tern_copy(copied)
                    copied += 1
            for q in range(copied, len(LOADS)):
                tern_copy(q)
            act.wait_ge(prep, 1)
            act.activation(fbT[:, :], x_bank[0][0:RANK, 0:RANK], ACT.Copy)
            act.activation(gate_col[:, :], x_bank[0][:, 32:33], ACT.Copy).then_inc(prep, 1)
            act.wait_ge(prep, 4)
            for col in (0, 32, 64):
                act.activation(a_stack[:, :, col:col + RANK], a_f32[:, :, :], ACT.Copy)
            act.activation(u_hi[:, :, :], u_nat[:, :, :], ACT.Copy).then_inc(prep, 1)
            act.wait_ge(prep, 7)
            for m in range(4):
                act.activation(u_stack[:, 512 * m:512 * m + 512], y_bank[m][:, :], ACT.Copy)
            act.activation(scale_row[:, :], x_bank[0][:, :], ACT.Copy).then_inc(prep, 1)

            def x_high(k, n):
                act.wait_ge(xm_full, n + 1)
                dst = xT_hi[:, k, :] if k < KT else z_sb[:, :]
                act.activation(dst, x_bank[k % 2][:, :], ACT.Copy).then_inc(xm_hi, 1)

            act.wait_ge(var_ready, 1)
            chain = Tally(act_self)
            ln_rstd(act, chain, ln).then_inc(rstd_ready, 1)
            for k in range(KT + 1):
                x_high(k, k)

            def program(steps, i):
                chain = Tally(act_self, i + 1)
                for s in steps:
                    if s[0] == "H":
                        b = s[1]
                        act.wait_ge(h_full, i * NB + b + 1)
                        act.activation(relu[:, b % 2, :], h_bank[b % 2][:, :], ACT.Relu, scale=scale_fc[:, b:b + 1]
                                       ).then_inc(relu_done, 1)
                        act.wait_ge(relu_done, i * NB + b + 1)
                        act.wait_ge(hid_ready, i * NB + b - 1 if b >= 2 else i * NB)
                        act.activation(act_sq[:, b % 2, :], relu[:, b % 2, :], ACT.Square).then_inc(sq_done, 1)
                    elif s[0] == "LN_STATS":
                        act.wait_ge(var_ready, i + 2)
                        ln_rstd(act, chain, ln).then_inc(rstd_ready, 1)
                    elif s[0] in ("XT", "Z"):
                        k = s[1] if s[0] == "XT" else KT
                        x_high(k, i * XJ + XJ + k)

            in_loop(act, program)

        @block.vector
        def _(dve):
            self_ = Tally(dve_self)

            def step(instruction):
                self_.inc(instruction)
                dve.wait_ge(dve_self, self_.now())

            for q, (kind, t, piece) in enumerate(LOADS):
                dve.wait_ge(sums_ready, row_loads(q)) if kind == "fc" else None
                if kind == "pr" and piece == 0:
                    dve.wait_ge(sums_ready, row_loads(q))
                col = t if kind == "fc" else NB + t
                scale = scale_fc[:, t:t + 1] if kind == "fc" else scale_pr[:, t:t + 1]
                if kind == "fc" or piece == 0:
                    total = parts[:, q:q + 1]
                    if kind == "pr":
                        step(dve.tensor_reduce(scale, parts[:, q:q + CHUNKS], AX.X, ALU.add))
                        total = scale
                    step(dve.tensor_scalar(scale, total, 1.0 / (D if kind == "fc" else HIDDEN), 1e-5, ALU.mult,
                                           ALU.max))
                    self_.inc(dve.tensor_scalar(half[:, col:col + 1], scale, 0.5, None, ALU.mult))
                    step(dve.tensor_scalar(neg_half[:, col:col + 1], scale, -0.5, None, ALU.mult))
                if q >= 2:
                    dve.wait_ge(tern_full, q - 1)
                step(dve.tensor_scalar(neg[:, q % 2, :], w_nat[:, q % 4, :], neg_half[:, col:col + 1], None, ALU.is_lt))
                dve.scalar_tensor_tensor(tern[:, q % 2, :], w_nat[:, q % 4, :], half[:, col:col + 1], neg[:, q % 2, :],
                                         ALU.is_gt, ALU.subtract).then_inc(tern_ready, 1)
            step(dve.reciprocal(inv_fc[:, :], scale_fc[:, :]))
            dve.wait_ge(small_loaded, 64)
            dve.wait_ge(prep, 3)
            dve.tensor_scalar(a_f32[:, :, :].rearrange("p k r -> p (k r)"), x_bank[1][:, 0:KT * RANK],
                              gate_col[:, 0:1], None, ALU.mult)
            for b in range(NB):
                last = dve.tensor_scalar(u_nat[:, b, :], u_nat[:, b, :], inv_fc[:, b:b + 1], None, ALU.mult)
            last.then_inc(prep, 1)
            dve.wait_ge(prep, 5)
            self_.inc(dve.tensor_tensor(a_stack[:, :, 96:96 + RANK], a_f32[:, :, :], a_stack[:, :, 0:RANK].bitcast(F32),
                                        ALU.subtract))
            step(dve.tensor_tensor(u_lo[:, :, :], u_nat[:, :, :], u_hi[:, :, :].bitcast(F32), ALU.subtract))
            for col, src in ((0, u_hi), (32, u_hi), (64, u_lo), (96, u_hi)):
                dve.tensor_copy(u_cols[:, :, col:col + RANK], src[:, :, :].bitcast(F32))
            for j in range(OT):
                last = dve.tensor_scalar(diag[:, j, :], ident[:, :], scale_pr[:, j:j + 1], None, ALU.mult)
            last.then_inc(prep, 1)

            def x_low(k, n):
                dve.wait_ge(xm_hi, n + 1)
                if k < KT:
                    dve.tensor_tensor(xT_lo[:, k, :], x_bank[k % 2][:, :], xT_hi[:, k, :].bitcast(F32), ALU.subtract
                                      ).then_inc(xm_free, 1)
                else:
                    dve.tensor_tensor(z_sb[32:64, :], x_bank[0][32:64, :], z_sb[32:64, :].bitcast(F32), ALU.subtract
                                      ).then_inc(xm_free, 1)

            setup = self_.now()
            dve.wait_ge(x2_loaded, 16)
            ln_stats(dve, self_, ln, x_in, dve_passed).then_inc(var_ready, 1)
            dve.wait_ge(rstd_ready, 1)
            ln_apply(dve, self_, ln, x_in, x_hat, xhat_ready)
            for k in range(KT + 1):
                x_low(k, k)
            assert self_.now() == setup + CHAIN0

            def program(steps, i):
                chain = Tally(dve_self, i * CHAIN + setup + CHAIN0)
                for s in steps:
                    if s[0] == "H":
                        b = s[1]
                        dve.wait_ge(sq_done, i * NB + b + 1)
                        dve.wait_ge(y_full, i * NB + max(b + 1 - RING, 0))
                        dve.tensor_copy(a_hi[:, b % RING, :], act_sq[:, b % 2, :]).then_inc(hid_hi, 1)
                        dve.wait_ge(hid_hi, i * NB + b + 1)
                        dve.tensor_tensor(a_lo[:, b % RING, :], act_sq[:, b % 2, :], a_hi[:, b % RING, :].bitcast(F32),
                                          ALU.subtract).then_inc(hid_ready, 1)
                    elif s[0] == "LN_STATS":
                        dve.wait_ge(x2_loaded, i * 16 + 32)
                        ln_stats(dve, chain, ln, x_in, dve_passed).then_inc(var_ready, 1)
                    elif s[0] == "LN_APPLY":
                        dve.wait_ge(rstd_ready, i + 2)
                        ln_apply(dve, chain, ln, x_in, x_hat, xhat_ready)
                    elif s[0] in ("XT", "Z"):
                        k = s[1] if s[0] == "XT" else KT
                        x_low(k, i * XJ + XJ + k)
                    elif s[0] == "RES":
                        j = s[1]
                        if j == 0:
                            dve.wait_ge(y_full, i * NB + NB)
                            dve.wait_ge(y_stored, i * 16 * TT)
                            dve.wait_ge(xres_ready, i * TT + TT)
                        dve.tensor_tensor(y_sb[:, j, :], y_bank[j][:, :], scale_row[:, :], ALU.mult
                                          ).then_inc(y_free, 1)
                        dve.wait_ge(y_free, i * TT + j + 1)
                        dve.tensor_tensor(y_sb[:, j, :], y_sb[:, j, :], x_res[:, j, :], ALU.add).then_inc(y_ready, 1)
                if steps is STEADY:
                    assert chain.local == CHAIN

            in_loop(dve, program)


def xattn_ffn_kernel(nc, x, ctx_1024, Wq, Wk, Wv, bv, Wo, bo, fast_b, w_fc, w_proj, u, v, gate, out):
    batches = x.shape[0]
    tiles = batches * x.shape[1] // P
    x2 = nc.dram_tensor("x2", [tiles, P, x.shape[2]], F32, kind="Internal").ap()
    attention_phase(nc, (x, ctx_1024, Wq, Wk, Wv, bv, Wo, bo, x2), batches)
    ffn_phase(nc, (x2, fast_b, w_fc, w_proj, u, v, gate, out.rearrange("b (j p) d -> (b j) p d", p=P)), batches)


_INS = ["x", "ctx_1024", "L0_xattn_Wq", "L0_xattn_Wk", "L0_xattn_Wv", "L0_xattn_bv", "L0_xattn_Wo", "L0_xattn_bo",
        "L0_ffn_fast_b", "L0_ffn_w_fc", "L0_ffn_w_proj", "L0_ffn_u", "L0_ffn_v", "L0_ffn_gate"]


def kernel(**inputs):
    import numpy as _np
    import concourse.bacc as _bacc
    from concourse.bass_utils import run_bass_kernel_spmd as _run

    nc = _bacc.Bacc("TRN2", target_bir_lowering=False, num_devices=1)
    arrays, args = {}, []
    for name in _INS:
        a = _np.ascontiguousarray(inputs[name])
        if a.ndim == 0:
            a = a.reshape(1, 1)
        arrays[f"in_{name}_dram"] = a
        args.append(nc.dram_tensor(f"in_{name}_dram", a.shape, mybir.dt.from_np(a.dtype), kind="ExternalInput").ap())
    shape = inputs["x"].shape
    args.append(nc.dram_tensor("out_0_dram", shape, F32, kind="ExternalOutput").ap())
    xattn_ffn_kernel(nc, *args)
    r = _run(nc, [arrays], core_ids=[0])
    return r.results[0]["out_0_dram"]
```

```python
from contextlib import ExitStack

import concourse.bass as bass
from concourse import mybir

F32 = mybir.dt.float32
F32R = mybir.dt.float32r
BF16 = mybir.dt.bfloat16
ALU = mybir.AluOpType
ACT = mybir.ActivationFunctionType
AX = mybir.AxisListType

P = 128
HEADS = 16
GROUPS = 4
GH = HEADS // GROUPS
EPS = 1e-5
MASKED = -1e30
UNITS = 10


MM_STEPS = ("W", "BIAS", "XT", "CT", "Q", "K", "V")
PV_ORDER = (0, 1, 3, 2)


def weave(units, fillers, rest=0):
    out, taken = [], 0
    for k, u in enumerate(units):
        out.append(u)
        due = min((k + 1) * len(fillers) // (len(units) - rest), len(fillers))
        out += fillers[taken:due]
        taken = due
    return out


def parts(*product):
    return [("PART", product[0], product[1], 0), ("PART", product[0], product[1], 1), product]


def setup_steps():
    return ([("W", w, k) for w in range(4) for k in range(4)] + [("BIAS",)]
            + [("LN_STATS", j) for j in range(4)] + [("LN_VAR",), ("LN_RSTD",)] + [("LN_APPLY", j) for j in range(4)]
            + [("XT", k) for k in range(4)] + [("Q", 0)] + [("CT", k) for k in range(4)]
            + [("K", 0), ("STACK", 0, 0), ("STACK", 0, 1)])


def batch_steps(more):
    def nxt(*steps):
        return list(steps) if more else []

    def score(kind, g, lo=0, hi=UNITS):
        return [(kind, g, k) for k in range(lo, hi)]

    def pv(g):
        return [("PV", g, r) for r in PV_ORDER]

    def stack(g):
        return [("STACK", g, 0), ("STACK", g, 1)]

    def norm(g):
        return [("NR", g, c) for c in range(4)] + [("NM", g, 0), ("NH", g, 0), ("NL", g, 0)]

    layernorm = ([("LN_STATS", j) for j in range(4)] + [("LN_VAR",), ("LN_RSTD",)]
                 + [("LN_APPLY", j) for j in range(4)])

    steps = [("XRES",), ("V", 0)]
    steps += weave(score("S", 0), parts("Q", 1) + parts("K", 1) + parts("V", 1))
    steps += [("STACK", 1, 0), ("M", 0), ("STACK", 1, 1), ("V", 2)] + nxt(("X_LOAD",))
    v3 = parts("V", 3)
    steps += weave(score("S", 1, 0, 3) + weave(score("T", 0), score("S", 1, 3)),
                   parts("Q", 2) + parts("K", 2) + [("STACK", 2, 0)], rest=4)
    steps += v3[:1] + [("M", 1), ("STACK", 2, 1)] + v3[1:] + pv(0) + nxt(*layernorm)
    steps += weave(score("T", 1, 0, 2) + weave(score("S", 2), score("T", 1, 2, 6) + [("NC", 0)] + score("T", 1, 6)),
                   parts("Q", 3) + parts("K", 3) + [("STACK", 3, 0)], rest=4)
    steps += nxt(("XT", 0)) + [("M", 2), ("STACK", 3, 1)]
    steps += weave(norm(0)[:4], pv(1)[:2]) + [("NM", 0, 0)] + nxt(("XT", 1)) + [("NH", 0, 0), ("NL", 0, 0)] + pv(1)[2:]
    q0 = parts("Q", 0)
    steps += weave(score("T", 2, 0, 4), nxt(("XT", 2), ("XT", 3))) + nxt(("C_LOAD",))
    steps += weave(weave(score("S", 3), score("T", 2, 4) + [("NC", 1)]), nxt(*q0[:2], ("Q", 0), ("CT", 2)))
    steps += nxt(("CT", 3)) + [("M", 3)] + pv(2) + norm(1)[:5]
    steps += score("T", 3, 0, 2) + norm(1)[5:] + score("T", 3, 2, 4)
    steps += weave(score("T", 3, 4), [("OA", j, g) for j in range(2) for g in range(2)])
    steps += [("NC", 2)] + [("OA", j, g) for j in range(2, 4) for g in range(2)] + norm(2)[:4]
    steps += pv(3)[:1] + nxt(("CT", 0)) + [("NM", 2, 0)] + pv(3)[1:2] + nxt(("CT", 1)) + norm(2)[5:] + pv(3)[2:]
    steps += [("NR", 3, 0), ("NM", 3, 0), ("NH", 3, 0), ("NR", 3, 1), ("NM", 3, 1), ("NL", 3, 0), ("NH", 3, 1),
              ("NR", 3, 2), ("NM", 3, 2), ("NL", 3, 1)]
    steps += nxt(("K", 0), *stack(0))
    steps += [("NH", 3, 2), ("NL", 3, 2), ("NR", 3, 3), ("NM", 3, 3), ("NH", 3, 3), ("NL", 3, 3)]
    steps += [("OC", j) for j in range(4)] + [("OB", j) for j in range(4)]
    return steps


def low_parts_later(steps):
    out, held = [], None
    for k, s in enumerate(steps):
        if s[0] in MM_STEPS + ("STACK", "M"):
            if held is not None:
                out.append(held)
            ahead = [x[0] for x in steps[k + 1:k + 4]]
            if s[0] in ("Q", "K", "V", "XT", "CT") and "S" in ahead and not any(
                    x in MM_STEPS for x in ahead[:ahead.index("S")]):
                held = s
                continue
            held = None
        out.append(s)
        if s[0] == "S" and held is not None:
            out.append(held)
            held = None
    assert held is None
    return out


def is_next(step, in_batch):
    return in_batch and (step[0] in ("LN_STATS", "LN_VAR", "LN_RSTD", "LN_APPLY", "XT", "CT")
                         or step[:2] in (("Q", 0), ("K", 0), ("STACK", 0)) or step[:3] == ("PART", "Q", 0))


def count_mm(steps):
    return sum(s[0] in MM_STEPS for s in steps)


def wait_alone(engine, passed, *waits):
    for sem, value in waits:
        engine.wait_ge(sem, value)
        engine.sem_inc(passed, 1)


class Tally:

    def __init__(self, sem, base=0):
        self.sem, self.base, self.local = sem, base, 0

    def inc(self, instruction):
        instruction.then_inc(self.sem, 1)
        self.local += 1

    def now(self):
        return self.base + self.local


def layernorm_buffers(sb, tt):
    shapes = {"stats": [P, tt, 6], "mean_var": [P, tt, 2], "v": [P, tt], "log": [P, tt], "y": [P, tt], "t": [P, tt],
              "rstd": [P, tt]}
    return {name: sb(f"ln_{name}", shape) for name, shape in shapes.items()}


def ln_stats(dve, chain, ln, rows, j):
    chain.inc(dve.bn_stats(ln["stats"][:, j, :], rows[:, j, :]))


def ln_var(dve, chain, ln, tt, passed):
    wait_alone(dve, passed, (chain.sem, chain.now()))
    for j in range(tt):
        chain.inc(dve.bn_aggr(ln["mean_var"][:, j, :], ln["stats"][:, j, :]))
    dve.wait_ge(chain.sem, chain.now())
    return dve.tensor_scalar(ln["v"][:, :], ln["mean_var"][:, :, 1], EPS, None, ALU.add)


def ln_rstd(act, chain, ln):
    chain.inc(act.activation(ln["log"][:, :], ln["v"][:, :], ACT.Ln))
    act.wait_ge(chain.sem, chain.now())
    return act.activation(ln["y"][:, :], ln["log"][:, :], ACT.Exp, scale=-0.5)


def ln_newton(dve, chain, ln):
    t, y, v, rstd = (ln[k][:, :] for k in ("t", "y", "v", "rstd"))
    for step in (lambda: dve.tensor_tensor(t, y, y, ALU.mult), lambda: dve.tensor_tensor(t, t, v, ALU.mult),
                 lambda: dve.tensor_scalar(t, t, -0.5, 1.5, ALU.mult, ALU.add),
                 lambda: dve.tensor_tensor(rstd, y, t, ALU.mult)):
        chain.inc(step())
        dve.wait_ge(chain.sem, chain.now())


def ln_apply(dve, ln, rows, x_hat, j, ready):
    dve.tensor_scalar(x_hat[:, j, :], rows[:, j, :], ln["mean_var"][:, j, 0:1], ln["rstd"][:, j:j + 1],
                      ALU.subtract, ALU.mult).then_inc(ready, 1)


def attention_phase(nc, dram, batches):
    x, ctx_in, Wq, Wk, Wv, bv, Wo, bo, x2_out = dram
    S, D = x.shape[1], x.shape[2]
    KT = D // P
    TT = S // P
    HD = D // HEADS
    SCALE = float(HD) ** -0.5
    assert (S, D, HD, KT, TT) == (512, 512, 32, 4, 4)

    SETUP, STEADY, LAST = setup_steps(), batch_steps(True), batch_steps(False)
    MM0, MMB = count_mm(SETUP), count_mm(STEADY)
    assert MMB % 2 == 0
    SB = TB = UNITS * GROUPS
    NORMS = GROUPS - 1 + TT

    with ExitStack() as c:
        def sb(name, shape, dt=F32):
            return c.enter_context(nc.sbuf_tensor(name, shape, dt))

        def sem(name):
            return c.enter_context(nc.semaphore(name))

        wT_hi = sb("wT_hi", [P, 4, KT, D], F32R)
        wT_lo = sb("wT_lo", [P, 4, KT, D], F32R)
        stack = [sb(f"stack{s}", [P, 2, GH, S], F32R) for s in range(2)]
        stage = sb("stage", [P, 4, S], F32R)
        probs = sb("probs", [P, UNITS, S])
        xT_hi = sb("xT_hi", [P, KT, S], F32R)
        xT_lo = sb("xT_lo", [P, KT, S], F32R)
        cT_hi = sb("cT_hi", [P, KT, S], F32R)
        cT_lo = sb("cT_lo", [P, KT, S], F32R)
        v_sb = sb("v_sb", [P, TT, D])
        x_in = sb("x_in", [P, TT, D])
        x_res = sb("x_res", [P, TT, D])
        xc_rows = sb("xc_rows", [P, TT, D])
        attn_hi = sb("attn_hi", [P, 2, S], F32R)
        attn_lo = sb("attn_lo", [P, 2, S], F32R)
        o_recip = sb("o_recip", [P, S])
        o_norm = sb("o_norm", [P, S])
        bias_sb = sb("bias_sb", [P, D])
        ident = sb("ident", [P, P])
        ident_bf = sb("ident_bf", [P, P], BF16)
        masks = sb("masks", [P, 2, P], BF16)
        ones = sb("ones", [P, P])
        maxima = sb("maxima", [P, P])
        m_stage = sb("m_stage", [16, 2, P], F32R)
        bv_col = sb("bv_col", [P, GROUPS])
        ln = layernorm_buffers(sb, TT)

        bank = [c.enter_context(nc.psum_tensor(f"bank{n}", [P, 512], F32)) for n in range(8)]
        mm_bank, s_bank, t_bank, o_bank, sum_bank = bank[0:2], bank[2:4], bank[4:6], bank[6], bank[7]

        w_loaded = [sem(f"w_loaded{n}") for n in range(4)]
        b_loaded = sem("b_loaded")
        x_loaded = sem("x_loaded")
        c_loaded = sem("c_loaded")
        consts_ready = sem("consts_ready")
        mm_full = sem("mm_full")
        mm_hi = sem("mm_hi")
        mm_free = sem("mm_free")
        s_full = sem("s_full")
        s_free = sem("s_free")
        m_full = sem("m_full")
        m_hi = sem("m_hi")
        m_free = sem("m_free")
        t_full = sem("t_full")
        exp_done = sem("exp_done")
        selected = sem("selected")
        pv_done = sem("pv_done")
        o_normed = sem("o_normed")
        o_copied = sem("o_copied")
        ot_hi = sem("ot_hi")
        ot_ready = sem("ot_ready")
        o_full = sem("o_full")
        o_free = sem("o_free")
        qk_stacked = [[sem(f"qk_stacked{s}{p}") for p in range(2)] for s in range(2)]
        m_stacked = [sem(f"m_stacked{s}") for s in range(2)]
        var_ready = sem("var_ready")
        rstd_ready = sem("rstd_ready")
        act_self = sem("act_self")
        dve_self = sem("dve_self")
        xhat_ready = sem("xhat_ready")
        xres_ready = sem("xres_ready")
        x2_stored = sem("x2_stored")
        sp_passed, pool_passed, dve_passed = sem("sp_passed"), sem("pool_passed"), sem("dve_passed")

        CONSTS = 11
        MM_BIAS = 17
        HI_SKIP = sum(s[0] == "V" for s in STEADY)
        CHAIN0, CHAIN = 12, 28

        block = c.enter_context(nc.Block())

        STACKED = (slice(0, 3, 2), slice(1, 3, 1), slice(0, 4, 3))
        QS, KS = 0, 1

        m_bank = s_bank[0]
        out_bank = (s_bank[0], s_bank[1], t_bank[0], t_bank[1])
        attn = [(cT_hi[:, g, :], cT_lo[:, g, :]) for g in range(2)]
        attn += [(attn_hi[:, g, :], attn_lo[:, g, :]) for g in range(2)]
        w_rows = (x_in[:, :, :], xc_rows[:, :, :], probs[:, 0:4, :], x_res[:, :, :])
        first_context = probs[:, 4:8, :]

        def norm_part(g, c):
            return (slice(P * c, P * c + P) if g == GROUPS - 1 else slice(0, S)), g + c

        def jobs(steps, first, parity):
            n = 0
            for s in steps:
                if s[0] in MM_STEPS:
                    yield s, first + n, mm_bank[(parity + n) % 2]
                    n += 1
                elif s[0] == "PART":
                    yield s, first + n, mm_bank[(parity + n) % 2]
                else:
                    yield s, None, None

        def in_loop(engine, program):
            program(SETUP, None, 0, 0)
            if batches > 1:
                with engine.Fori(0, batches - 1, 1) as i:
                    program(STEADY, i, i * MMB + MM0, MM0 % 2)
            program(LAST, batches - 1, (batches - 1) * MMB + MM0, MM0 % 2)

        def batch_of(step, i):
            return 0 if i is None else i + 1 if is_next(step, True) else i

        def staged(eng, sems, g, b, each):
            if g > 0:
                eng.wait_ge(sems[(g - 1) % 2], (b * 2 + (g - 1) // 2 + 1) * each)
            elif not isinstance(b, int) or b > 0:
                eng.wait_ge(sems[1], b * 2 * each)

        @block.sync
        def _(sp):
            def stack_qk(g, b, pair):
                for h in (2 * pair, 2 * pair + 1):
                    for r, pick in enumerate(STACKED):
                        sp.dma_start(stack[g % 2][32 * r:32 * r + 32, :, h, :].bitcast(F32),
                                     stage[32 * h:32 * h + 32, pick, :].bitcast(F32)
                                     ).then_inc(qk_stacked[g % 2][pair], 16)

            def program(steps, i, first, parity):
                if i is None:
                    for w, (dst, src) in enumerate(zip(w_rows, (Wq, Wk, Wv, Wo))):
                        sp.dma_start(dst, src.rearrange("(j p) d -> p j d", p=P)).then_inc(w_loaded[w], 16)
                    sp.dma_start(first_context, ctx_in[0].rearrange("(j p) d -> p j d", p=P)).then_inc(c_loaded, 16)
                    with nc.allow_non_contiguous_dma(reason="512 values, once"):
                        sp.dma_start(bv_col[:, :], bv.rearrange("(g p) -> p g", p=P)).then_inc(b_loaded, 16)
                    sp.dma_start(o_recip[0:1, :], bo.rearrange("(a d) -> a d", a=1)).then_inc(b_loaded, 16)
                for s, n, _ in jobs(steps, first, parity):
                    b = batch_of(s, i)
                    if s == ("W", 1, 0) and i is None:
                        sp.wait_ge(mm_full, 4)
                        sp.dma_start(x_in[:, :, :], x[0].rearrange("(j p) d -> p j d", p=P)).then_inc(x_loaded, 16)
                    elif s[0] == "X_LOAD":
                        wait_alone(sp, sp_passed, (xres_ready, i * TT + TT))
                        sp.dma_start(x_in[:, :, :], x[bass.ds(i + 1, 1)].rearrange("a (j p) d -> p (a j) d", p=P)
                                     ).then_inc(x_loaded, 16)
                    elif s == ("XT", 3):
                        last_xt = n
                    elif s[0] == "C_LOAD":
                        wait_alone(sp, sp_passed, (mm_full, last_xt + 1))
                        sp.dma_start(xc_rows[:, :, :], ctx_in[bass.ds(i + 1, 1)].rearrange("a (j p) d -> p (a j) d", p=P)
                                     ).then_inc(c_loaded, 16)
                    elif s[0] == "K":
                        k_job[s[1]] = n
                    elif s[0] == "STACK":
                        g, pair = s[1:]
                        if pair == 0:
                            wait_alone(sp, sp_passed, (mm_free, k_job[g] + 1))
                        if g >= 2:
                            wait_alone(sp, sp_passed, (t_full, i * TB + UNITS * (g - 2) + 5 * pair + 5))
                        stack_qk(g, b, pair)
                    elif s[0] == "M":
                        g = s[1]
                        wait_alone(sp, sp_passed, (m_free, i * GROUPS + g + 1))
                        for part in range(2):
                            sp.dma_start(stack[g % 2][96 + part:97 + part, 0, :, :].bitcast(F32)
                                         .rearrange("p h (r s) -> p (h r) s", s=P),
                                         m_stage[:, part, :].bitcast(F32)).then_inc(m_stacked[g % 2], 16)
                    elif s[0] == "OB":
                        wait_alone(sp, sp_passed, (o_free, i * TT + s[1] + 1))
                        sp.dma_start(x2_out[bass.ds(i * TT + s[1], 1)].rearrange("a p d -> p (a d)"),
                                     x_res[:, s[1], :]).then_inc(x2_stored, 16)
                if steps is LAST:
                    sp.wait_ge(x2_stored, 16 * TT * batches)

            k_job = {}
            in_loop(sp, program)

        @block.gpsimd
        def _(pool):
            consts = Tally(consts_ready)
            consts.inc(pool.memset(ident[:, :], 0.0))
            consts.inc(pool.memset(ident_bf[:, :], 0.0))
            consts.inc(pool.memset(masks[:, :, :], 0.0))
            consts.inc(pool.memset(ones[:, :], 1.0))
            consts.inc(pool.memset(maxima[:, :], 0.0))
            pool.wait_ge(consts_ready, consts.now())
            for m in (ident, ident_bf):
                consts.inc(pool.affine_select(out=m[:, :], in_=m[:, :], compare_op=ALU.not_equal, fill=1.0,
                                              base=0, pattern=[[-1, P]], channel_multiplier=1))
            consts.inc(pool.affine_select(out=masks[:, 0, :], in_=masks[:, 0, :], compare_op=ALU.is_ge, fill=MASKED,
                                          base=0, pattern=[[-(P + 1), P]], channel_multiplier=P))
            consts.inc(pool.affine_select(out=masks[:, 1, :], in_=masks[:, 1, :], compare_op=ALU.is_ge, fill=MASKED,
                                          base=-1, pattern=[[-1, P]], channel_multiplier=1))
            for s in range(2):
                pool.wait_ge(consts_ready, consts.now())
                consts.inc(pool.memset(stack[s][96:98, KS, :, :].bitcast(F32), -1.0))
            pool.wait_ge(consts_ready, CONSTS)

            def select(view, first_block):
                count = view.shape[1] if len(view.shape) == 3 else None
                return pool.affine_select(out=view, in_=view, compare_op=ALU.is_ge, fill=0.0,
                                          base=0 if first_block else -1,
                                          pattern=([[0, count]] if count else []) + [[P if first_block else 1, P]],
                                          channel_multiplier=-(P + 1) if first_block else -1)

            def program(steps, i, first, parity):
                for s, n, _ in jobs(steps, first, parity):
                    if s[0] == "XRES":
                        pool.wait_ge(x_loaded, i * 16 + 16)
                        pool.wait_ge(mm_free, first)
                        pool.wait_ge(x2_stored, i * 16 * TT)
                        for j in range(TT):
                            pool.tensor_tensor(x_res[:, j, :], x_in[:, j, :], bias_sb[:, :], ALU.add
                                               ).then_inc(xres_ready, 1)
                    elif s[0] == "T":
                        k = s[2]
                        wait_alone(pool, pool_passed, (exp_done, i * TB + UNITS * s[1] + k + 1))
                        blocks = probs[:, k, :].rearrange("p (c x) -> p c x", x=P)
                        view = probs[:, k, 0:P] if k % 5 in (0, 2) else blocks[:, 0:4:3 if k % 5 < 4 else 2, :]
                        select(view, k % 5 in (0, 2)).then_inc(selected, 1)

            in_loop(pool, program)

        @block.tensor
        def _(pe):
            def split_product(out, a_hi, a_lo, b_hi, b_lo, tiles, part=None):
                pairs = [(a, b, k) for k in tiles for a, b in ((a_hi, b_hi), (a_hi, b_lo), (a_lo, b_hi))]
                third = len(pairs) // 3
                start, stop = (0, len(pairs)) if part is None else (part * third, part * third + third)
                for m, (a, b, k) in list(enumerate(pairs))[start:stop]:
                    last = pe.matmul(out, a(k), b(k), start=m == 0, stop=m == len(pairs) - 1)
                return last

            def s_unit(g, k, out):
                st = stack[g % 2]
                pair, u = divmod(k, 5)

                def block(h, r, t1, cols):
                    pe.matmul(out[:, cols:cols + t1], st[0:96, QS, h, P * r:P * r + P], st[0:96, KS, h, 0:t1],
                              start=True, stop=False)
                    return pe.matmul(out[:, cols + t1 - P:cols + t1], ident_bf[:, :], masks[:, min(r, 1), :],
                                     start=False, stop=True)

                if u < 4 and u % 2 == 0:
                    return block(2 * pair + u // 2, 3, 512, 0)
                if u < 4:
                    block(2 * pair + u // 2, 2, 384, 0)
                    return block(2 * pair + u // 2, 0, 128, 384)
                block(2 * pair, 1, 256, 0)
                return block(2 * pair + 1, 1, 256, 256)

            def t_unit(g, k, out):
                st = stack[g % 2]
                pair, u = divmod(k, 5)

                def block(h, r, cols):
                    return pe.matmul(out[:, cols:cols + S - P * r], st[0:98, KS, h, P * r:P * r + P],
                                     st[0:98, QS, h, P * r:S], start=True, stop=True)

                if u < 4 and u % 2 == 0:
                    return block(2 * pair + u // 2, 0, 0)
                if u < 4:
                    block(2 * pair + u // 2, 1, 0)
                    return block(2 * pair + u // 2, 3, 384)
                block(2 * pair, 2, 0)
                return block(2 * pair + 1, 2, 256)

            def pv(g, r):
                for target in (o_bank, sum_bank):
                    for h in range(GH):
                        base = 5 * (h // 2)
                        unit, cols = {0: (base + 2 * (h % 2), 0), 1: (base + 2 * (h % 2) + 1, 0),
                                      3: (base + 2 * (h % 2) + 1, 384), 2: (base + 4, 256 * (h % 2))}[r]
                        weights = (v_sb[:, r, (GH * g + h) * HD:(GH * g + h + 1) * HD] if target is o_bank
                                   else ones[:, 0:HD])
                        last = pe.matmul(target[HD * h:HD * h + HD, P * r:S], weights,
                                         probs[:, unit, cols:cols + S - P * r], start=r == PV_ORDER[0],
                                         stop=r == PV_ORDER[-1])
                return last

            def out_part(j, groups):
                pairs = [(part, w, g) for g in groups for part, w in ((0, wT_hi), (0, wT_lo), (1, wT_hi))]
                for m, (part, w, g) in enumerate(pairs):
                    last = pe.matmul(out_bank[j][:, :], attn[g][part][:, P * j:P * j + P], w[:, 3, g, :],
                                     start=g == 0 and m == 0, stop=g == GROUPS - 1 and m == len(pairs) - 1)
                return last

            def program(steps, i, first, parity):
                for s, n, out in jobs(steps, first, parity):
                    b = batch_of(s, i)
                    part = None
                    if s[0] == "PART":
                        part, s = s[3], s[1:3]
                        begun[s] = True
                    elif begun.pop(s, False):
                        part = 2
                    if n is not None and part in (None, 0) and not (isinstance(n, int) and n < 2):
                        pe.wait_ge(mm_free, n - 1)
                    if s[0] == "W":
                        if s[2] == 0:
                            pe.wait_ge(w_loaded[s[1]], 16)
                            pe.wait_ge(consts_ready, CONSTS)
                        src = w_rows[s[1]]
                        for j in range(4):
                            last = pe.transpose(out[:, P * j:P * j + P], src[:, j, P * s[2]:P * s[2] + P], ident[:, :])
                        last.then_inc(mm_full, 1)
                    elif s[0] == "BIAS":
                        pe.wait_ge(ot_ready, 1)
                        split_product(out[:, :], lambda k: stage[:, 0, P * k:P * k + P],
                                      lambda k: stage[:, 1, P * k:P * k + P],
                                      lambda k: wT_hi[:, 3, k, :], lambda k: wT_lo[:, 3, k, :], range(4))
                        pe.matmul(out[:, :], ones[0:1, :], o_recip[0:1, :], start=False, stop=True,
                                  skip_group_check=True).then_inc(mm_full, 1)
                    elif s[0] in ("XT", "CT"):
                        if s == ("XT", 0):
                            pe.wait_ge(xhat_ready, b * TT + TT)
                        elif s == ("CT", 0 if i is None else 2):
                            pe.wait_ge(c_loaded, b * 16 + 16)
                        src = first_context if s[0] == "CT" and i is None else xc_rows
                        for j in range(TT):
                            last = pe.transpose(out[:, P * j:P * j + P], src[:, j, P * s[1]:P * s[1] + P], ident[:, :])
                        last.then_inc(mm_full, 1)
                    elif s[0] in ("Q", "K"):
                        w, t_hi, t_lo = (0, xT_hi, xT_lo) if s[0] == "Q" else (1, cT_hi, cT_lo)
                        if s[1] == 0 and part in (None, 0):
                            pe.wait_ge(mm_free, transposed[s[0]] + 1)
                        g = s[1]
                        last = split_product(out[:, :], lambda k: wT_hi[:, w, k, P * g:P * g + P],
                                             lambda k: wT_lo[:, w, k, P * g:P * g + P],
                                             lambda k: t_hi[:, k, :], lambda k: t_lo[:, k, :], range(KT), part)
                        if part in (None, 2):
                            last.then_inc(mm_full, 1)
                    elif s[0] == "V":
                        j = s[1]
                        last = split_product(out[:, :], lambda k: cT_hi[:, k, P * j:P * j + P],
                                             lambda k: cT_lo[:, k, P * j:P * j + P],
                                             lambda k: wT_hi[:, 2, k, :], lambda k: wT_lo[:, 2, k, :], range(KT), part)
                        if part in (None, 2):
                            last.then_inc(mm_full, 1)
                        v_job[s[1]] = n
                    elif s[0] == "S":
                        u = UNITS * s[1] + s[2]
                        if u == 0:
                            pe.wait_ge(o_free, i * TT)
                        if s[2] in (0, 5):
                            pe.wait_ge(qk_stacked[s[1] % 2][s[2] // 5], (i * 2 + s[1] // 2 + 1) * 96)
                        if s[2] == 0 and s[1] > 0:
                            pe.wait_ge(m_free, i * GROUPS + s[1])
                        pe.wait_ge(s_free, i * SB + max(u - 1, 0))
                        s_unit(s[1], s[2], s_bank[u % 2]).then_inc(s_full, 1)
                    elif s[0] == "M":
                        pe.wait_ge(s_free, i * SB + UNITS * s[1] + UNITS)
                        pe.transpose(m_bank[:, 0:P], maxima[:, :], ident[:, :]).then_inc(m_full, 1)
                    elif s[0] == "T":
                        u = UNITS * s[1] + s[2]
                        if u == 0:
                            pe.wait_ge(o_free, i * TT)
                        if s[2] == 0:
                            pe.wait_ge(m_stacked[s[1] % 2], (i * 2 + s[1] // 2 + 1) * 32)
                        if u >= 2:
                            pe.wait_ge(exp_done, i * TB + u - 1)
                        t_unit(s[1], s[2], t_bank[u % 2]).then_inc(t_full, 1)
                    elif s[0] == "PV":
                        g, r = s[1:]
                        if r == PV_ORDER[0]:
                            pe.wait_ge(selected, i * TB + UNITS * g + UNITS)
                            if g > 0:
                                pe.wait_ge(o_copied, i * (GROUPS - 1) + g)
                            else:
                                pe.wait_ge(o_normed, i * NORMS + 1)
                        if g == 0:
                            pe.wait_ge(mm_free, v_job[r] + 1)
                        last = pv(g, r)
                        if r == PV_ORDER[-1]:
                            last.then_inc(pv_done, 1)
                    elif s[0] == "OA":
                        if s[1:] == (0, 0):
                            pe.wait_ge(ot_ready, i * NORMS + 3)
                            pe.wait_ge(m_free, i * GROUPS + GROUPS)
                        if s[1:] == (2, 0):
                            pe.wait_ge(exp_done, i * TB + TB)
                        out_part(s[1], (s[2],))
                    elif s[0] == "OC":
                        if s[1] == 0:
                            pe.wait_ge(ot_ready, i * NORMS + 4)
                        out_part(s[1], (2,))
                    elif s[0] == "OB":
                        pe.wait_ge(ot_ready, i * NORMS + 5 + s[1])
                        out_part(s[1], (3,)).then_inc(o_full, 1)
                    if s[0] in ("XT", "CT"):
                        transposed["Q" if s[0] == "XT" else "K"] = n

            transposed, begun, v_job = {}, {}, {}
            in_loop(pe, program)

        @block.scalar
        def _(act):
            def program(steps, i, first, parity):
                chain = Tally(act_self, 0 if i is None else i + 1)
                for s, n, out in jobs(steps, first, parity):
                    b = batch_of(s, i)
                    if s[0] == "M":
                        act.wait_ge(m_full, i * GROUPS + s[1] + 1)
                        staged(act, m_stacked, s[1], b, 32)
                        act.activation(m_stage[:, 0, :], m_bank[0:16, 0:P], ACT.Copy).then_inc(m_hi, 1)
                    elif s[0] in ("W", "XT", "CT", "Q", "K"):
                        act.wait_ge(mm_full, n + 1)
                        if s[0] == "W":
                            dst = wT_hi[:, s[1], s[2], :]
                        elif s[0] == "XT":
                            dst = xT_hi[:, s[1], :]
                        elif s[0] == "CT":
                            dst = cT_hi[:, s[1], :]
                        else:
                            dst = stage[:, 0 if s[0] == "Q" else 2, :]
                            for p in range(2):
                                staged(act, [q[p] for q in qk_stacked], s[1], b, 96)
                        act.activation(dst, out[:, :], ACT.Copy).then_inc(mm_hi, 1)
                    elif s[0] == "BIAS":
                        act.wait_ge(o_normed, 1)
                        act.activation(stage[:, 0, :], o_norm[:, :], ACT.Copy).then_inc(ot_hi, 1)
                        act.wait_ge(mm_full, n + 1)
                        act.activation(bias_sb[:, :], out[:, :], ACT.Copy).then_inc(mm_hi, 1)
                    elif s[0] == "LN_VAR":
                        act.wait_ge(var_ready, b + 1)
                        ln_rstd(act, chain, ln).then_inc(rstd_ready, 1)
                    elif s[0] == "T":
                        u = UNITS * s[1] + s[2]
                        act.wait_ge(t_full, i * TB + u + 1)
                        act.activation(probs[:, s[2], :], t_bank[u % 2][:, :], ACT.Exp, scale=SCALE
                                       ).then_inc(exp_done, 1)
                    elif s[0] == "NC":
                        g = s[1]
                        act.wait_ge(pv_done, i * GROUPS + g + 1)
                        act.wait_ge(ot_ready, i * NORMS + g + 1)
                        act.activation(o_recip[:, :], sum_bank[:, :], ACT.Copy)
                        act.activation(o_norm[:, :], o_bank[:, :], ACT.Copy).then_inc(o_copied, 1)
                    elif s[0] == "NH":
                        cols, number = norm_part(*s[1:])
                        act.wait_ge(o_normed, i * NORMS + number + 2)
                        act.activation(attn[s[1]][0][:, cols], o_norm[:, cols], ACT.Copy).then_inc(ot_hi, 1)

            in_loop(act, program)

        @block.vector
        def _(dve):
            def program(steps, i, first, parity):
                chain = Tally(dve_self, 0 if i is None else i * CHAIN + CHAIN0)
                hi = 0 if i is None else i * (MMB - HI_SKIP) + MM0
                highs = 0
                for s, n, out in jobs(low_parts_later(steps), first, parity):
                    b = batch_of(s, i)
                    if s[0] == "M":
                        dve.wait_ge(m_hi, i * GROUPS + s[1] + 1)
                        dve.tensor_tensor(m_stage[:, 1, :], m_bank[0:16, 0:P], m_stage[:, 0, :].bitcast(F32),
                                          ALU.subtract).then_inc(m_free, 1)
                    elif s[0] in ("W", "XT", "CT", "Q", "K"):
                        a_hi, a_lo = {"W": lambda: (wT_hi[:, s[1], s[2], :], wT_lo[:, s[1], s[2], :]),
                                  "XT": lambda: (xT_hi[:, s[1], :], xT_lo[:, s[1], :]),
                                  "CT": lambda: (cT_hi[:, s[1], :], cT_lo[:, s[1], :]),
                                  "Q": lambda: (stage[:, 0, :], stage[:, 1, :]),
                                  "K": lambda: (stage[:, 2, :], stage[:, 3, :])}[s[0]]()
                        highs += 1
                        dve.wait_ge(mm_hi, hi + highs)
                        dve.tensor_tensor(a_lo, out[:, :], a_hi.bitcast(F32), ALU.subtract
                                          ).then_inc(mm_free, 1)
                    elif s[0] == "BIAS":
                        dve.wait_ge(b_loaded, 32)
                        dve.wait_ge(consts_ready, CONSTS)
                        for g in range(GROUPS):
                            last = dve.tensor_scalar(o_norm[:, P * g:P * g + P], ones[:, :], bv_col[:, g:g + 1], None,
                                                     ALU.mult)
                        last.then_inc(o_normed, 1)
                        dve.wait_ge(ot_hi, 1)
                        dve.tensor_tensor(stage[:, 1, :], o_norm[:, :], stage[:, 0, :].bitcast(F32), ALU.subtract
                                          ).then_inc(ot_ready, 1)
                        highs += 1
                        dve.wait_ge(mm_hi, hi + highs)
                        dve.tensor_copy(o_norm[:, :], bias_sb[:, :]).then_inc(mm_free, 1)
                    elif s[0] == "V":
                        dve.wait_ge(mm_full, n + 1)
                        dve.tensor_copy(v_sb[:, s[1], :], out[:, :]).then_inc(mm_free, 1)
                    elif s[0] == "S":
                        u = UNITS * s[1] + s[2]
                        bank_u = s_bank[u % 2]
                        pair, k = divmod(s[2], 5)
                        dve.wait_ge(s_full, i * SB + u + 1)
                        if k < 4 and k % 2 == 0:
                            col = 4 * (2 * pair + k // 2)
                            last = dve.tensor_reduce(maxima[:, col + 3:col + 4], bank_u[:, :], AX.X, ALU.max)
                        elif k < 4:
                            col = 4 * (2 * pair + k // 2)
                            dve.tensor_reduce(maxima[:, col + 2:col + 3], bank_u[:, 0:384], AX.X, ALU.max)
                            last = dve.tensor_reduce(maxima[:, col:col + 1], bank_u[:, 384:512], AX.X, ALU.max)
                        else:
                            col = 8 * pair + 1
                            last = dve.tensor_reduce(maxima[:, col:col + 5:4],
                                                     bank_u[:, :].rearrange("p (h t) -> p h t", h=2), AX.X, ALU.max)
                        last.then_inc(s_free, 1)
                    elif s[0] == "LN_STATS":
                        if s[1] == 0:
                            dve.wait_ge(x_loaded, b * 16 + 16)
                        ln_stats(dve, chain, ln, x_in, s[1])
                    elif s[0] == "LN_VAR":
                        ln_var(dve, chain, ln, TT, dve_passed).then_inc(var_ready, 1)
                    elif s[0] == "LN_RSTD":
                        dve.wait_ge(rstd_ready, b + 1)
                        ln_newton(dve, chain, ln)
                    elif s[0] == "LN_APPLY":
                        ln_apply(dve, ln, x_in, xc_rows, s[1], xhat_ready)
                    elif s[0] == "NR":
                        g, c = s[1:]
                        if c == 0 and g < GROUPS - 1:
                            dve.wait_ge(o_copied, i * (GROUPS - 1) + g + 1)
                        elif c == 0:
                            dve.wait_ge(pv_done, i * GROUPS + g + 1)
                        src = sum_bank if g == GROUPS - 1 else o_recip
                        chain.inc(dve.reciprocal(o_recip[:, P * c:P * c + P], src[:, P * c:P * c + P]))
                    elif s[0] == "NM":
                        cols, _number = norm_part(*s[1:])
                        dve.wait_ge(dve_self, chain.now())
                        src = o_bank if s[1] == GROUPS - 1 else o_norm
                        dve.tensor_tensor(o_norm[:, cols], src[:, cols], o_recip[:, cols], ALU.mult
                                          ).then_inc(o_normed, 1)
                    elif s[0] == "NL":
                        cols, number = norm_part(*s[1:])
                        hi_part, lo_part = attn[s[1]]
                        dve.wait_ge(ot_hi, i * NORMS + number + 2)
                        dve.tensor_tensor(lo_part[:, cols], o_norm[:, cols], hi_part[:, cols].bitcast(F32),
                                          ALU.subtract).then_inc(ot_ready, 1)
                    elif s[0] == "OB":
                        j = s[1]
                        dve.wait_ge(o_full, i * TT + j + 1)
                        if j == 0:
                            dve.wait_ge(xres_ready, i * TT + TT)
                        dve.tensor_tensor(x_res[:, j, :], out_bank[j][:, :], x_res[:, j, :], ALU.add
                                          ).then_inc(o_free, 1)
                if steps is SETUP:
                    assert chain.local == CHAIN0
                elif steps is STEADY:
                    assert chain.local == CHAIN

            in_loop(dve, program)




HIDDEN_LAG = 4


def ffn_steps(blocks, more):
    steps = [("COPY",)]
    for b in range(blocks):
        steps.append(("H", b))
        if b >= HIDDEN_LAG:
            steps.append(("Y", b - HIDDEN_LAG))
        if more and b == 5:
            steps.append(("LN_STATS",))
        if more and b == 7:
            steps.append(("LN_APPLY",))
    for m, b in enumerate(range(blocks - HIDDEN_LAG, blocks)):
        if more:
            steps.append(("XT", m))
        steps.append(("Y", b))
    steps += [("RES", j) for j in range(4)]
    if more:
        steps.insert(len(steps) - 4, ("Z",))
    return steps


def ffn_phase(nc, dram, batches):
    x2_in, fast_b, w_fc, w_proj, u_in, v_in, gate, y_out = dram
    HIDDEN, D = w_fc.shape
    RANK = u_in.shape[1]
    KT, NB, TT, OT = D // P, HIDDEN // P, 4, D // P
    S = TT * P
    CHUNKS = HIDDEN // D
    assert RANK <= 32 and D == 512 and KT == 4 and HIDDEN_LAG == KT
    STEADY, LAST = ffn_steps(NB, True), ffn_steps(NB, False)
    XJ = KT + 1
    RING = 8

    with ExitStack() as c:
        def sb(name, shape, dt=F32):
            return c.enter_context(nc.sbuf_tensor(name, shape, dt))

        def sem(name):
            return c.enter_context(nc.semaphore(name))

        fcT = sb("fcT", [P, KT, HIDDEN], F32R)
        projT = sb("projT", [P, NB, D], F32R)
        a_stack = sb("a_stack", [P, KT, P], F32R)
        u_stack = sb("u_stack", [P, HIDDEN], F32R)
        w_nat = sb("w_nat", [P, 4, D])
        tern = sb("tern", [P, 2, D], BF16)
        neg = sb("neg", [P, 2, D], BF16)
        u_nat = sb("u_nat", [P, NB, RANK])
        u_hi = sb("u_hi", [P, NB, RANK], F32R)
        u_lo = sb("u_lo", [P, NB, RANK], F32R)
        u_cols = sb("u_cols", [P, NB, P])
        v_sb = sb("v_rows", [RANK, D])
        fb_sb = sb("fb_sb", [RANK, RANK])
        fbT = sb("fbT", [RANK, RANK])
        gate_sb = sb("gate_sb", [1, 1])
        gate_col = sb("gate_col", [P, 1])
        a_f32 = sb("a_f32", [P, KT, RANK])
        scale_fc = sb("scale_fc", [P, NB])
        scale_pr = sb("scale_pr", [P, OT])
        parts = sb("parts", [P, NB + OT * CHUNKS])
        half = sb("half", [P, NB + OT])
        neg_half = sb("neg_half", [P, NB + OT])
        inv_fc = sb("inv_fc", [P, NB])
        diag = sb("diag", [P, OT, P])
        scale_row = sb("scale_row", [P, D])
        junk = sb("junk", [P, D])
        ident = sb("ident2", [P, P])
        ident_bf = sb("ident2_bf", [P, P], BF16)
        ones = sb("ones2", [P, P])
        xT_hi = sb("x2T_hi", [P, KT, S], F32R)
        xT_lo = sb("x2T_lo", [P, KT, S], F32R)
        x_in = sb("x2_in_sb", [P, TT, D])
        x_res = sb("x2_res", [P, TT, D])
        x_hat = sb("x2_hat", [P, TT, D])
        y_sb = sb("y_sb", [P, TT, D])
        z_sb = sb("z_sb", [P, S], F32R)
        relu = sb("relu", [P, 2, S])
        act_sq = sb("act_sq", [P, 2, S])
        a_hi = sb("a_hi", [P, RING, S], F32R)
        a_lo = sb("a_lo", [P, RING, S], F32R)
        ln = layernorm_buffers(lambda n, s: sb(f"{n}2", s), TT)

        h_bank = [c.enter_context(nc.psum_tensor(f"h_bank{n}", [P, 512], F32)) for n in range(2)]
        x_bank = [c.enter_context(nc.psum_tensor(f"x_bank{n}", [P, 512], F32)) for n in range(2)]
        y_bank = [c.enter_context(nc.psum_tensor(f"y_bank{n}", [P, 512], F32)) for n in range(4)]

        wn_loaded = [sem(f"wn_loaded{n}") for n in range(4)]
        small_loaded = sem("small_loaded")
        consts_ready = sem("consts2_ready")
        sums_ready = sem("sums_ready")
        tern_ready = sem("tern_ready")
        tern_full = sem("tern_full")
        tern_out = sem("tern_out")
        prep = sem("prep")
        x2_loaded = sem("x2_loaded")
        h_full = sem("h_full")
        relu_done = sem("relu_done")
        sq_done = sem("sq_done")
        hid_hi = sem("hid_hi")
        hid_ready = sem("hid_ready")
        y_full = sem("y_full")
        y_free = sem("y_free")
        y_ready = sem("y_ready")
        y_stored = sem("y_stored")
        xm_full = sem("xm_full")
        xm_hi = sem("xm_hi")
        xm_free = sem("xm_free")
        var_ready = sem("var2_ready")
        rstd_ready = sem("rstd2_ready")
        act_self = sem("act2_self")
        dve_self = sem("dve2_self")
        xhat_ready = sem("xhat2_ready")
        xres_ready = sem("xres2_ready")
        sp_passed, pool_passed, dve_passed = sem("sp2_passed"), sem("pool2_passed"), sem("dve2_passed")

        LOADS = [("fc", t, 0) for t in range(NB)] + [("pr", t, q) for t in range(OT) for q in range(CHUNKS)]
        CONSTS = 7
        CHAIN0 = CHAIN = 12

        block = c.enter_context(nc.Block())

        def in_loop(engine, program):
            if batches > 1:
                with engine.Fori(0, batches - 1, 1) as i:
                    program(STEADY, i)
            program(LAST, batches - 1)

        def row_loads(q):
            kind, t, _ = LOADS[q]
            return q + 1 if kind == "fc" else NB + (t + 1) * CHUNKS

        @block.sync
        def _(sp):
            nc_ctx = nc.allow_non_contiguous_dma(reason="rows of 16 values, once")
            with nc_ctx:
                sp.dma_start(u_nat[:, :, :], u_in.rearrange("(b p) r -> p b r", p=P)).then_inc(small_loaded, 16)
                sp.dma_start(v_sb[:, :], v_in).then_inc(small_loaded, 16)
                sp.dma_start(fb_sb[:, :], fast_b).then_inc(small_loaded, 16)
                sp.dma_start(gate_sb[:, :], gate).then_inc(small_loaded, 16)
            for q, (kind, t, piece) in enumerate(LOADS):
                if q >= 4:
                    sp.wait_ge(tern_ready, q - 3)
                rows = w_fc if kind == "fc" else w_proj
                sp.dma_start(w_nat[:, q % 4, :], rows[P * t:P * t + P, D * piece:D * piece + D]
                             ).then_inc(wn_loaded[q % 4], 16)
            sp.dma_start(x_in[:, :, :], x2_in[0:TT].rearrange("j p d -> p j d")).then_inc(x2_loaded, 16)

            def program(steps, i):
                for s in steps:
                    if s[0] == "COPY" and steps is STEADY:
                        wait_alone(sp, sp_passed, (xres_ready, i * TT + TT))
                        wait_alone(sp, sp_passed, (xm_free, i * XJ + XJ))
                        sp.dma_start(x_in[:, :, :], x2_in[bass.ds(i * TT + TT, TT)].rearrange("j p d -> p j d")
                                     ).then_inc(x2_loaded, 16)
                    elif s[0] == "RES":
                        wait_alone(sp, sp_passed, (y_ready, i * TT + s[1] + 1))
                        sp.dma_start(y_out[bass.ds(i * TT + s[1], 1)].rearrange("a p d -> p (a d)"), y_sb[:, s[1], :]
                                     ).then_inc(y_stored, 16)

            in_loop(sp, program)
            sp.wait_ge(y_stored, 16 * TT * batches)

        @block.gpsimd
        def _(pool):
            consts = Tally(consts_ready)
            consts.inc(pool.memset(ident[:, :], 0.0))
            consts.inc(pool.memset(ident_bf[:, :], 0.0))
            consts.inc(pool.memset(ones[:, :], 1.0))
            consts.inc(pool.memset(u_cols[:, :, :], 0.0))
            consts.inc(pool.memset(a_stack[:, :, :].bitcast(F32), 0.0))
            pool.wait_ge(consts_ready, consts.now())
            for m in (ident, ident_bf):
                consts.inc(pool.affine_select(out=m[:, :], in_=m[:, :], compare_op=ALU.not_equal, fill=1.0,
                                              base=0, pattern=[[-1, P]], channel_multiplier=1))

            def program(steps, i):
                for s in steps:
                    if s[0] == "COPY":
                        wait_alone(pool, pool_passed, (x2_loaded, i * 16 + 16), (y_ready, i * TT))
                        for j in range(TT):
                            pool.tensor_copy(x_res[:, j, :], x_in[:, j, :]).then_inc(xres_ready, 1)

            in_loop(pool, program)

        @block.tensor
        def _(pe):
            def transposed(target, src, k):
                for j in range(TT):
                    last = pe.transpose(target[:, P * j:P * j + P], src[:, j, P * k:P * k + P], ident[:, :])
                return last

            pe.wait_ge(consts_ready, CONSTS)
            for q in range(len(LOADS)):
                pe.wait_ge(tern_ready, q + 1)
                if q >= 2:
                    pe.wait_ge(tern_out, q - 1)
                out = h_bank[q % 2][:, 0:256].bitcast(BF16)
                for k in range(4):
                    last = pe.transpose(out[:, P * k:P * k + P], tern[:, q % 2, P * k:P * k + P], ident_bf[:, :])
                last.then_inc(tern_full, 1)
            pe.wait_ge(small_loaded, 64)
            pe.matmul(x_bank[0][0:RANK, 0:RANK], fb_sb[:, :], ident[0:RANK, 0:RANK], start=True, stop=True)
            pe.matmul(x_bank[0][:, 32:33], ones[0:1, :], gate_sb[:, :], start=True, stop=True).then_inc(prep, 1)
            pe.wait_ge(prep, 2)
            for k in range(KT):
                last = pe.matmul(x_bank[1][:, RANK * k:RANK * k + RANK], v_sb[:, P * k:P * k + P], fbT[:, :],
                                 start=True, stop=True)
            last.then_inc(prep, 1)
            pe.wait_ge(prep, 6)
            for b in range(NB):
                last = pe.transpose(y_bank[b // 4][:, P * (b % 4):P * (b % 4) + P], u_cols[:, b, :], ident[:, :])
            for j in range(OT):
                last = pe.matmul(x_bank[0][:, P * j:P * j + P], ones[:, :], diag[:, j, :], start=True, stop=True)
            last.then_inc(prep, 1)
            pe.wait_ge(prep, 8)
            pe.wait_ge(tern_out, len(LOADS))

            def z_product(n):
                pe.wait_ge(xm_free, n)
                for k in range(KT):
                    for part in (xT_hi, xT_lo):
                        last = pe.matmul(x_bank[0][:, :], a_stack[:, k, :], part[:, k, :],
                                         start=k == 0 and part is xT_hi, stop=k == KT - 1 and part is xT_lo)
                last.then_inc(xm_full, 1)

            pe.wait_ge(xhat_ready, TT)
            for k in range(KT):
                if k >= 2:
                    pe.wait_ge(xm_free, k - 1)
                transposed(x_bank[k % 2], x_hat, k).then_inc(xm_full, 1)
            z_product(KT)

            def program(steps, i):
                for s in steps:
                    if s[0] == "H":
                        b = s[1]
                        if b >= 2:
                            pe.wait_ge(relu_done, i * NB + b - 1)
                        else:
                            pe.wait_ge(relu_done, i * NB)
                        cols = slice(P * b, P * b + P)
                        for k in range(KT):
                            pe.matmul(h_bank[b % 2][:, :], fcT[:, k, cols], xT_hi[:, k, :], start=k == 0, stop=False)
                            pe.matmul(h_bank[b % 2][:, :], fcT[:, k, cols], xT_lo[:, k, :], start=False, stop=False)
                        if b == 0:
                            pe.wait_ge(xm_free, i * XJ + XJ)
                        pe.matmul(h_bank[b % 2][:, :], u_stack[:, cols], z_sb[:, :], start=False, stop=True
                                  ).then_inc(h_full, 1)
                    elif s[0] == "Y":
                        b = s[1]
                        pe.wait_ge(hid_ready, i * NB + b + 1)
                        if b == 0:
                            pe.wait_ge(y_free, i * TT)
                        for j in range(TT):
                            pe.matmul(y_bank[j][:, :], a_hi[:, b % RING, P * j:P * j + P], projT[:, b, :],
                                      start=b == 0, stop=False)
                            last = pe.matmul(y_bank[j][:, :], a_lo[:, b % RING, P * j:P * j + P], projT[:, b, :],
                                             start=False, stop=b == NB - 1)
                        last.then_inc(y_full, 1)
                    elif s[0] == "XT":
                        k = s[1]
                        n = i * XJ + XJ + k
                        if k == 0:
                            pe.wait_ge(xhat_ready, i * TT + 2 * TT)
                        pe.wait_ge(xm_free, n if k == 0 else n - 1)
                        transposed(x_bank[k % 2], x_hat, k).then_inc(xm_full, 1)
                    elif s[0] == "Z":
                        z_product(i * XJ + XJ + KT)

            in_loop(pe, program)

        @block.scalar
        def _(act):
            def row_sum(q):
                act.wait_ge(wn_loaded[q % 4], q // 4 * 16 + 16)
                act.activation(junk[:, :], w_nat[:, q % 4, :], ACT.Abs, accum_out=parts[:, q:q + 1]
                               ).then_inc(sums_ready, 1)
                act.wait_ge(sums_ready, q + 1)

            def tern_copy(q):
                kind, t, piece = LOADS[q]
                act.wait_ge(tern_full, q + 1)
                src = h_bank[q % 2][:, 0:256].bitcast(BF16).rearrange("p (k c) -> p k c", k=4)
                dst = fcT[:, :, P * t:P * t + P] if kind == "fc" else projT[:, 4 * piece:4 * piece + 4,
                                                                          P * t:P * t + P]
                act.activation(dst, src, ACT.Copy).then_inc(tern_out, 1)

            copied = 0
            for q in range(len(LOADS)):
                row_sum(q)
                while copied < len(LOADS) and row_loads(copied) <= q - 1:
                    tern_copy(copied)
                    copied += 1
            for q in range(copied, len(LOADS)):
                tern_copy(q)
            act.wait_ge(prep, 1)
            act.activation(fbT[:, :], x_bank[0][0:RANK, 0:RANK], ACT.Copy)
            act.activation(gate_col[:, :], x_bank[0][:, 32:33], ACT.Copy).then_inc(prep, 1)
            act.wait_ge(prep, 4)
            for col in (0, 32, 64):
                act.activation(a_stack[:, :, col:col + RANK], a_f32[:, :, :], ACT.Copy)
            act.activation(u_hi[:, :, :], u_nat[:, :, :], ACT.Copy).then_inc(prep, 1)
            act.wait_ge(prep, 7)
            for m in range(4):
                act.activation(u_stack[:, 512 * m:512 * m + 512], y_bank[m][:, :], ACT.Copy)
            act.activation(scale_row[:, :], x_bank[0][:, :], ACT.Copy).then_inc(prep, 1)

            def x_high(k, n):
                act.wait_ge(xm_full, n + 1)
                dst = xT_hi[:, k, :] if k < KT else z_sb[:, :]
                act.activation(dst, x_bank[k % 2][:, :], ACT.Copy).then_inc(xm_hi, 1)

            act.wait_ge(var_ready, 1)
            chain = Tally(act_self)
            ln_rstd(act, chain, ln).then_inc(rstd_ready, 1)
            for k in range(KT + 1):
                x_high(k, k)

            def program(steps, i):
                chain = Tally(act_self, i + 1)
                for s in steps:
                    if s[0] == "H":
                        b = s[1]
                        act.wait_ge(h_full, i * NB + b + 1)
                        act.activation(relu[:, b % 2, :], h_bank[b % 2][:, :], ACT.Relu, scale=scale_fc[:, b:b + 1]
                                       ).then_inc(relu_done, 1)
                        act.wait_ge(relu_done, i * NB + b + 1)
                        act.wait_ge(hid_ready, i * NB + b - 1 if b >= 2 else i * NB)
                        act.activation(act_sq[:, b % 2, :], relu[:, b % 2, :], ACT.Square).then_inc(sq_done, 1)
                    elif s[0] == "LN_STATS":
                        act.wait_ge(var_ready, i + 2)
                        ln_rstd(act, chain, ln).then_inc(rstd_ready, 1)
                    elif s[0] in ("XT", "Z"):
                        k = s[1] if s[0] == "XT" else KT
                        x_high(k, i * XJ + XJ + k)

            in_loop(act, program)

        @block.vector
        def _(dve):
            self_ = Tally(dve_self)

            def step(instruction):
                self_.inc(instruction)
                dve.wait_ge(dve_self, self_.now())

            for q, (kind, t, piece) in enumerate(LOADS):
                dve.wait_ge(sums_ready, row_loads(q)) if kind == "fc" else None
                if kind == "pr" and piece == 0:
                    dve.wait_ge(sums_ready, row_loads(q))
                col = t if kind == "fc" else NB + t
                scale = scale_fc[:, t:t + 1] if kind == "fc" else scale_pr[:, t:t + 1]
                if kind == "fc" or piece == 0:
                    total = parts[:, q:q + 1]
                    if kind == "pr":
                        step(dve.tensor_reduce(scale, parts[:, q:q + CHUNKS], AX.X, ALU.add))
                        total = scale
                    step(dve.tensor_scalar(scale, total, 1.0 / (D if kind == "fc" else HIDDEN), 1e-5, ALU.mult,
                                           ALU.max))
                    self_.inc(dve.tensor_scalar(half[:, col:col + 1], scale, 0.5, None, ALU.mult))
                    step(dve.tensor_scalar(neg_half[:, col:col + 1], scale, -0.5, None, ALU.mult))
                if q >= 2:
                    dve.wait_ge(tern_full, q - 1)
                step(dve.tensor_scalar(neg[:, q % 2, :], w_nat[:, q % 4, :], neg_half[:, col:col + 1], None, ALU.is_lt))
                dve.scalar_tensor_tensor(tern[:, q % 2, :], w_nat[:, q % 4, :], half[:, col:col + 1], neg[:, q % 2, :],
                                         ALU.is_gt, ALU.subtract).then_inc(tern_ready, 1)
            step(dve.reciprocal(inv_fc[:, :], scale_fc[:, :]))
            dve.wait_ge(small_loaded, 64)
            dve.wait_ge(prep, 3)
            dve.tensor_scalar(a_f32[:, :, :].rearrange("p k r -> p (k r)"), x_bank[1][:, 0:KT * RANK],
                              gate_col[:, 0:1], None, ALU.mult)
            for b in range(NB):
                last = dve.tensor_scalar(u_nat[:, b, :], u_nat[:, b, :], inv_fc[:, b:b + 1], None, ALU.mult)
            last.then_inc(prep, 1)
            dve.wait_ge(prep, 5)
            self_.inc(dve.tensor_tensor(a_stack[:, :, 96:96 + RANK], a_f32[:, :, :], a_stack[:, :, 0:RANK].bitcast(F32),
                                        ALU.subtract))
            step(dve.tensor_tensor(u_lo[:, :, :], u_nat[:, :, :], u_hi[:, :, :].bitcast(F32), ALU.subtract))
            for col, src in ((0, u_hi), (32, u_hi), (64, u_lo), (96, u_hi)):
                dve.tensor_copy(u_cols[:, :, col:col + RANK], src[:, :, :].bitcast(F32))
            for j in range(OT):
                last = dve.tensor_scalar(diag[:, j, :], ident[:, :], scale_pr[:, j:j + 1], None, ALU.mult)
            last.then_inc(prep, 1)

            def x_low(k, n):
                dve.wait_ge(xm_hi, n + 1)
                if k < KT:
                    dve.tensor_tensor(xT_lo[:, k, :], x_bank[k % 2][:, :], xT_hi[:, k, :].bitcast(F32), ALU.subtract
                                      ).then_inc(xm_free, 1)
                else:
                    dve.tensor_tensor(z_sb[32:64, :], x_bank[0][32:64, :], z_sb[32:64, :].bitcast(F32), ALU.subtract
                                      ).then_inc(xm_free, 1)

            setup = self_.now()
            dve.wait_ge(x2_loaded, 16)
            for j in range(TT):
                ln_stats(dve, self_, ln, x_in, j)
            ln_var(dve, self_, ln, TT, dve_passed).then_inc(var_ready, 1)
            dve.wait_ge(rstd_ready, 1)
            ln_newton(dve, self_, ln)
            for j in range(TT):
                ln_apply(dve, ln, x_in, x_hat, j, xhat_ready)
            for k in range(KT + 1):
                x_low(k, k)
            assert self_.now() == setup + CHAIN0

            def program(steps, i):
                chain = Tally(dve_self, i * CHAIN + setup + CHAIN0)
                for s in steps:
                    if s[0] == "H":
                        b = s[1]
                        dve.wait_ge(sq_done, i * NB + b + 1)
                        dve.wait_ge(y_full, i * NB + max(b + 1 - RING, 0))
                        dve.tensor_copy(a_hi[:, b % RING, :], act_sq[:, b % 2, :]).then_inc(hid_hi, 1)
                        dve.wait_ge(hid_hi, i * NB + b + 1)
                        dve.tensor_tensor(a_lo[:, b % RING, :], act_sq[:, b % 2, :], a_hi[:, b % RING, :].bitcast(F32),
                                          ALU.subtract).then_inc(hid_ready, 1)
                    elif s[0] == "LN_STATS":
                        dve.wait_ge(x2_loaded, i * 16 + 32)
                        for j in range(TT):
                            ln_stats(dve, chain, ln, x_in, j)
                        ln_var(dve, chain, ln, TT, dve_passed).then_inc(var_ready, 1)
                    elif s[0] == "LN_APPLY":
                        dve.wait_ge(rstd_ready, i + 2)
                        ln_newton(dve, chain, ln)
                        for j in range(TT):
                            ln_apply(dve, ln, x_in, x_hat, j, xhat_ready)
                    elif s[0] in ("XT", "Z"):
                        k = s[1] if s[0] == "XT" else KT
                        x_low(k, i * XJ + XJ + k)
                    elif s[0] == "RES":
                        j = s[1]
                        if j == 0:
                            dve.wait_ge(y_full, i * NB + NB)
                            dve.wait_ge(y_stored, i * 16 * TT)
                            dve.wait_ge(xres_ready, i * TT + TT)
                        dve.tensor_tensor(y_sb[:, j, :], y_bank[j][:, :], scale_row[:, :], ALU.mult
                                          ).then_inc(y_free, 1)
                        dve.wait_ge(y_free, i * TT + j + 1)
                        dve.tensor_tensor(y_sb[:, j, :], y_sb[:, j, :], x_res[:, j, :], ALU.add).then_inc(y_ready, 1)
                if steps is STEADY:
                    assert chain.local == CHAIN

            in_loop(dve, program)


def xattn_ffn_kernel(nc, x, ctx_1024, Wq, Wk, Wv, bv, Wo, bo, fast_b, w_fc, w_proj, u, v, gate, out):
    batches = x.shape[0]
    tiles = batches * x.shape[1] // P
    x2 = nc.dram_tensor("x2", [tiles, P, x.shape[2]], F32, kind="Internal").ap()
    attention_phase(nc, (x, ctx_1024, Wq, Wk, Wv, bv, Wo, bo, x2), batches)
    ffn_phase(nc, (x2, fast_b, w_fc, w_proj, u, v, gate, out.rearrange("b (j p) d -> (b j) p d", p=P)), batches)


_INS = ["x", "ctx_1024", "L0_xattn_Wq", "L0_xattn_Wk", "L0_xattn_Wv", "L0_xattn_bv", "L0_xattn_Wo", "L0_xattn_bo",
        "L0_ffn_fast_b", "L0_ffn_w_fc", "L0_ffn_w_proj", "L0_ffn_u", "L0_ffn_v", "L0_ffn_gate"]


def kernel(**inputs):
    import numpy as _np
    import concourse.bacc as _bacc
    from concourse.bass_utils import run_bass_kernel_spmd as _run

    nc = _bacc.Bacc("TRN2", target_bir_lowering=False, num_devices=1)
    arrays, args = {}, []
    for name in _INS:
        a = _np.ascontiguousarray(inputs[name])
        if a.ndim == 0:
            a = a.reshape(1, 1)
        arrays[f"in_{name}_dram"] = a
        args.append(nc.dram_tensor(f"in_{name}_dram", a.shape, mybir.dt.from_np(a.dtype), kind="ExternalInput").ap())
    shape = inputs["x"].shape
    args.append(nc.dram_tensor("out_0_dram", shape, F32, kind="ExternalOutput").ap())
    xattn_ffn_kernel(nc, *args)
    r = _run(nc, [arrays], core_ids=[0])
    return r.results[0]["out_0_dram"]
```

```python
from contextlib import ExitStack

import concourse.bass as bass
from concourse import mybir

F32 = mybir.dt.float32
F32R = mybir.dt.float32r
BF16 = mybir.dt.bfloat16
ALU = mybir.AluOpType
ACT = mybir.ActivationFunctionType
AX = mybir.AxisListType

P = 128
HEADS = 16
GROUPS = 4
GH = HEADS // GROUPS
EPS = 1e-5
MASKED = -1e30
UNITS = 10


MM_STEPS = ("W", "BIAS", "XT", "CT", "Q", "K", "V")
PV_ORDER = (0, 1, 3, 2)


def weave(units, fillers, rest=0):
    out, taken = [], 0
    for k, u in enumerate(units):
        out.append(u)
        due = min((k + 1) * len(fillers) // (len(units) - rest), len(fillers))
        out += fillers[taken:due]
        taken = due
    return out


def parts(*product):
    return [("PART", product[0], product[1], 0), ("PART", product[0], product[1], 1), product]


def setup_steps():
    def w(n):
        return [("W", n, k) for k in range(4)]

    return ([("LN_STATS", j) for j in range(4)] + [("LN_VAR",)] + w(0) + [("LN_RSTD",)]
            + [("LN_APPLY", j) for j in range(4)] + [("CT", k) for k in range(4)] + [("XT", k) for k in range(4)]
            + w(1) + [("Q", 0), ("K", 0), ("STACK", 0, 0), ("STACK", 0, 1), ("BV",)] + w(2) + w(3) + [("BIAS",)])


def batch_steps(more):
    def nxt(*steps):
        return list(steps) if more else []

    def score(kind, g, lo=0, hi=UNITS):
        return [(kind, g, k) for k in range(lo, hi)]

    def pv(g):
        return [("PV", g, r) for r in PV_ORDER]

    def stack(g):
        return [("STACK", g, 0), ("STACK", g, 1)]

    def norm(g):
        return [("NR", g, c) for c in range(4)] + [("NM", g, 0), ("NH", g, 0), ("NL", g, 0)]

    layernorm = ([("LN_STATS", j) for j in range(4)] + [("LN_VAR",), ("LN_RSTD",)]
                 + [("LN_APPLY", j) for j in range(4)])

    def with_copy(g, at):
        return score("T", g, 0, at) + [("NC", g - 1)] + score("T", g, at)

    steps = [("XRES",), ("V", 0)]
    steps += weave(score("S", 0), parts("Q", 1) + parts("K", 1) + [("STACK", 1, 0)] + parts("V", 1))
    steps += [("M", 0), ("STACK", 1, 1), ("V", 2)] + nxt(("X_LOAD",))
    v3 = parts("V", 3)
    steps += weave(score("S", 1, 0, 2) + weave(score("T", 0), score("S", 1, 2)),
                   parts("Q", 2) + parts("K", 2) + [("STACK", 2, 0)], rest=6)
    steps += v3[0:2] + [("M", 1), ("STACK", 2, 1)] + v3[2:] + pv(0) + nxt(*layernorm)
    t1 = with_copy(1, 6)
    steps += weave(t1[:4] + weave(score("S", 2), t1[4:]), parts("Q", 3) + parts("K", 3) + [("STACK", 3, 0)], rest=4)
    steps += nxt(("XT", 0)) + [("M", 2), ("STACK", 3, 1)] + weave(norm(0)[:4], pv(1)[:2])
    steps += [("NM", 0, 0)] + nxt(("XT", 1)) + [("NH", 0, 0), ("NL", 0, 0)] + pv(1)[2:]
    t2, ct = with_copy(2, 6), nxt(("CT", 2), ("CT", 3))
    steps += weave(t2[:2], nxt(("XT", 2), ("XT", 3))) + nxt(("C_LOAD",))
    steps += weave(weave(score("S", 3), t2[2:]), (parts("Q", 0) if more else []) + ct[:1], rest=2)
    steps += ct[1:] + [("M", 3)] + pv(2) + norm(1)
    steps += score("T", 3, 0, 4) + weave(score("T", 3, 4), [("OA", j, g) for j in range(2) for g in range(2)])
    steps += [("NC", 2)] + [("OA", j, g) for j in range(2, 4) for g in range(2)] + norm(2)[:4]
    steps += pv(3)[:1] + nxt(("CT", 0)) + [("NM", 2, 0)] + pv(3)[1:2] + nxt(("CT", 1)) + norm(2)[5:] + pv(3)[2:]
    steps += [("NR", 3, 0), ("NM", 3, 0), ("NH", 3, 0), ("NR", 3, 1), ("NM", 3, 1), ("NL", 3, 0), ("NH", 3, 1),
              ("NR", 3, 2), ("NM", 3, 2), ("NL", 3, 1)]
    steps += nxt(("K", 0), *stack(0))
    steps += [("NH", 3, 2), ("NL", 3, 2), ("NR", 3, 3), ("NM", 3, 3), ("NH", 3, 3), ("NL", 3, 3)]
    steps += [("OC", j) for j in range(4)] + [("OB", j) for j in range(4)]
    return steps


def low_parts_later(steps):
    out, held = [], None
    for k, s in enumerate(steps):
        if s[0] in MM_STEPS + ("STACK", "M"):
            if held is not None:
                out.append(held)
            ahead = [x[0] for x in steps[k + 1:k + 4]]
            if s[0] in ("Q", "K", "V", "XT", "CT") and "S" in ahead and not any(
                    x in MM_STEPS for x in ahead[:ahead.index("S")]):
                held = s
                continue
            held = None
        out.append(s)
        if s[0] == "S" and held is not None:
            out.append(held)
            held = None
    assert held is None
    return out


def is_next(step, in_batch):
    return in_batch and (step[0] in ("LN_STATS", "LN_VAR", "LN_RSTD", "LN_APPLY", "XT", "CT")
                         or step[:2] in (("Q", 0), ("K", 0), ("STACK", 0)) or step[:3] == ("PART", "Q", 0))


def count_mm(steps):
    return sum(s[0] in MM_STEPS for s in steps)


def wait_alone(engine, passed, *waits):
    for sem, value in waits:
        engine.wait_ge(sem, value)
        engine.sem_inc(passed, 1)


START = 1


class Tally:

    def __init__(self, sem, base=0):
        self.sem, self.base, self.local = sem, base, 0

    def inc(self, instruction):
        instruction.then_inc(self.sem, 1)
        self.local += 1

    def now(self):
        return self.base + self.local


def layernorm_buffers(sb, tt):
    shapes = {"stats": [P, tt, 6], "mean_var": [P, tt, 2], "v": [P, tt], "log": [P, tt], "y": [P, tt], "t": [P, tt],
              "rstd": [P, tt]}
    return {name: sb(f"ln_{name}", shape) for name, shape in shapes.items()}


def ln_stats(dve, chain, ln, rows, j):
    chain.inc(dve.bn_stats(ln["stats"][:, j, :], rows[:, j, :]))


def ln_var(dve, chain, ln, tt, passed):
    wait_alone(dve, passed, (chain.sem, chain.now()))
    for j in range(tt):
        chain.inc(dve.bn_aggr(ln["mean_var"][:, j, :], ln["stats"][:, j, :]))
    dve.wait_ge(chain.sem, chain.now())
    return dve.tensor_scalar(ln["v"][:, :], ln["mean_var"][:, :, 1], EPS, None, ALU.add)


def ln_rstd(act, chain, ln):
    chain.inc(act.activation(ln["log"][:, :], ln["v"][:, :], ACT.Ln))
    act.wait_ge(chain.sem, chain.now())
    return act.activation(ln["y"][:, :], ln["log"][:, :], ACT.Exp, scale=-0.5)


def ln_newton(dve, chain, ln):
    t, y, v, rstd = (ln[k][:, :] for k in ("t", "y", "v", "rstd"))
    for step in (lambda: dve.tensor_tensor(t, y, y, ALU.mult), lambda: dve.tensor_tensor(t, t, v, ALU.mult),
                 lambda: dve.tensor_scalar(t, t, -0.5, 1.5, ALU.mult, ALU.add),
                 lambda: dve.tensor_tensor(rstd, y, t, ALU.mult)):
        chain.inc(step())
        dve.wait_ge(chain.sem, chain.now())


def ln_apply(dve, ln, rows, x_hat, j, ready):
    dve.tensor_scalar(x_hat[:, j, :], rows[:, j, :], ln["mean_var"][:, j, 0:1], ln["rstd"][:, j:j + 1],
                      ALU.subtract, ALU.mult).then_inc(ready, 1)


def attention_phase(nc, dram, batches):
    x, ctx_in, Wq, Wk, Wv, bv, Wo, bo, x2_out = dram
    S, D = x.shape[1], x.shape[2]
    KT = D // P
    TT = S // P
    HD = D // HEADS
    SCALE = float(HD) ** -0.5
    assert (S, D, HD, KT, TT) == (512, 512, 32, 4, 4)

    SETUP, STEADY, LAST = setup_steps(), batch_steps(True), batch_steps(False)
    MM0, MMB = count_mm(SETUP), count_mm(STEADY)
    assert MMB % 2 == 0
    SB = TB = UNITS * GROUPS
    NORMS = GROUPS - 1 + TT

    with ExitStack() as c:
        def sb(name, shape, dt=F32):
            return c.enter_context(nc.sbuf_tensor(name, shape, dt))

        def sem(name):
            return c.enter_context(nc.semaphore(name))

        wT_hi = sb("wT_hi", [P, 4, KT, D], F32R)
        wT_lo = sb("wT_lo", [P, 4, KT, D], F32R)
        stack = [sb(f"stack{s}", [P, 2, GH, S], F32R) for s in range(2)]
        stage = sb("stage", [P, 4, S], F32R)
        probs = sb("probs", [P, UNITS, S])
        xT_hi = sb("xT_hi", [P, KT, S], F32R)
        xT_lo = sb("xT_lo", [P, KT, S], F32R)
        cT_hi = sb("cT_hi", [P, KT, S], F32R)
        cT_lo = sb("cT_lo", [P, KT, S], F32R)
        v_sb = sb("v_sb", [P, TT, D])
        x_in = sb("x_in", [P, TT, D])
        x_res = sb("x_res", [P, TT, D])
        xc_rows = sb("xc_rows", [P, TT, D])
        attn_hi = sb("attn_hi", [P, 2, S], F32R)
        attn_lo = sb("attn_lo", [P, 2, S], F32R)
        o_recip = sb("o_recip", [P, S])
        o_norm = sb("o_norm", [P, S])
        bias_sb = sb("bias_sb", [P, D])
        ident = sb("ident", [P, P])
        ident_bf = sb("ident_bf", [P, P], BF16)
        masks = sb("masks", [P, 3, P], BF16)
        ones = sb("ones", [P, P])
        maxima = sb("maxima", [P, P])
        m_stage = sb("m_stage", [16, 2, P], F32R)
        bv_col = sb("bv_col", [P, GROUPS])
        ln = layernorm_buffers(sb, TT)

        bank = [c.enter_context(nc.psum_tensor(f"bank{n}", [P, 512], F32)) for n in range(8)]
        mm_bank, s_bank, t_bank, o_bank, sum_bank = bank[0:2], bank[2:4], bank[4:6], bank[6], bank[7]

        w_loaded = [sem(f"w_loaded{n}") for n in range(4)]
        b_loaded = sem("b_loaded")
        x_loaded = sem("x_loaded")
        c_loaded = sem("c_loaded")
        consts_ready = sem("consts_ready")
        mm_full = sem("mm_full")
        mm_hi = sem("mm_hi")
        mm_free = sem("mm_free")
        s_full = sem("s_full")
        s_free = sem("s_free")
        m_full = sem("m_full")
        m_hi = sem("m_hi")
        m_free = sem("m_free")
        t_full = sem("t_full")
        exp_done = sem("exp_done")
        selected = sem("selected")
        pv_done = sem("pv_done")
        o_normed = sem("o_normed")
        o_copied = sem("o_copied")
        ot_hi = sem("ot_hi")
        ot_ready = sem("ot_ready")
        o_full = sem("o_full")
        o_free = sem("o_free")
        qk_stacked = [[sem(f"qk_stacked{s}{p}") for p in range(2)] for s in range(2)]
        m_stacked = [sem(f"m_stacked{s}") for s in range(2)]
        var_ready = sem("var_ready")
        rstd_ready = sem("rstd_ready")
        act_self = sem("act_self")
        dve_self = sem("dve_self")
        xhat_ready = sem("xhat_ready")
        xres_ready = sem("xres_ready")
        x2_stored = sem("x2_stored")
        sp_passed, pool_passed, dve_passed = sem("sp_passed"), sem("pool_passed"), sem("dve_passed")

        CONSTS = 12
        HI_SKIP = sum(s[0] == "V" for s in STEADY)
        CHAIN0, CHAIN = 12, 28

        block = c.enter_context(nc.Block())

        STACKED = (slice(0, 3, 2), slice(1, 3, 1), slice(0, 4, 3))
        QS, KS = 0, 1

        m_bank = s_bank[0]
        out_bank = (s_bank[0], s_bank[1], t_bank[0], t_bank[1])
        attn = [(cT_hi[:, g, :], cT_lo[:, g, :]) for g in range(2)]
        attn += [(attn_hi[:, g, :], attn_lo[:, g, :]) for g in range(2)]
        w_rows = (v_sb[:, :, :], x_res[:, :, :], probs[:, 0:4, :], v_sb[:, :, :])
        first_context = probs[:, 4:8, :]

        def norm_part(g, c):
            return (slice(P * c, P * c + P) if g == GROUPS - 1 else slice(0, S)), g + c

        def jobs(steps, first, parity):
            ring = mm_bank + s_bank if steps[0] == SETUP[0] else mm_bank
            n = 0
            for s in steps:
                if s[0] in MM_STEPS:
                    yield s, first + n, ring[(parity + n) % len(ring)]
                    n += 1
                elif s[0] == "PART":
                    yield s, first + n, ring[(parity + n) % len(ring)]
                else:
                    yield s, None, None

        def in_loop(engine, program):
            program(SETUP, None, 0, 0)
            if batches > 1:
                with engine.Fori(0, batches - 1, 1) as i:
                    program(STEADY, i, i * MMB + MM0, MM0 % 2)
            program(LAST, batches - 1, (batches - 1) * MMB + MM0, MM0 % 2)

        def batch_of(step, i):
            return 0 if i is None else i + 1 if is_next(step, True) else i

        def staged(eng, sems, g, b, each):
            if g > 0:
                eng.wait_ge(sems[(g - 1) % 2], (b * 2 + (g - 1) // 2 + 1) * each)
            elif not isinstance(b, int) or b > 0:
                eng.wait_ge(sems[1], b * 2 * each)

        @block.sync
        def _(sp):
            def stack_qk(g, b, pair):
                for h in (2 * pair, 2 * pair + 1):
                    for r, pick in enumerate(STACKED):
                        sp.dma_start(stack[g % 2][32 * r:32 * r + 32, :, h, :].bitcast(F32),
                                     stage[32 * h:32 * h + 32, pick, :].bitcast(F32)
                                     ).then_inc(qk_stacked[g % 2][pair], 16)

            def program(steps, i, first, parity):
                if i is None:
                    for dst, src, loaded in (
                            (x_in[:, :, :], x[0], x_loaded), (w_rows[0], Wq, w_loaded[0]),
                            (first_context, ctx_in[0], c_loaded), (w_rows[1], Wk, w_loaded[1]),
                            (w_rows[2], Wv, w_loaded[2])):
                        sp.dma_start(dst, src.rearrange("(j p) d -> p j d", p=P)).then_inc(loaded, 16)
                    with nc.allow_non_contiguous_dma(reason="512 values, once"):
                        sp.dma_start(bv_col[:, :], bv.rearrange("(g p) -> p g", p=P)).then_inc(b_loaded, 16)
                    sp.dma_start(o_recip[0:1, :], bo.rearrange("(a d) -> a d", a=1)).then_inc(b_loaded, 16)
                for s, n, _ in jobs(steps, first, parity):
                    b = batch_of(s, i)
                    if s == ("W", 1, 0) and i is None:
                        sp.wait_ge(mm_full, 4)
                        sp.dma_start(w_rows[3], Wo.rearrange("(j p) d -> p j d", p=P)).then_inc(w_loaded[3], 16)
                    elif s[0] == "X_LOAD":
                        wait_alone(sp, sp_passed, (xres_ready, i * TT + TT))
                        sp.dma_start(x_in[:, :, :], x[bass.ds(i + 1, 1)].rearrange("a (j p) d -> p (a j) d", p=P)
                                     ).then_inc(x_loaded, 16)
                    elif s == ("XT", 3):
                        last_xt = n
                    elif s[0] == "C_LOAD":
                        wait_alone(sp, sp_passed, (mm_full, last_xt + 1))
                        sp.dma_start(xc_rows[:, :, :], ctx_in[bass.ds(i + 1, 1)].rearrange("a (j p) d -> p (a j) d", p=P)
                                     ).then_inc(c_loaded, 16)
                    elif s[0] in ("Q", "K"):
                        staged_job[s[1]] = n
                    elif s[0] == "STACK":
                        g, pair = s[1:]
                        if pair == 0:
                            wait_alone(sp, sp_passed, (mm_free, staged_job[g] + 1))
                        if g >= 2:
                            wait_alone(sp, sp_passed, (t_full, i * TB + UNITS * (g - 2) + 5 * pair + 5))
                        stack_qk(g, b, pair)
                    elif s[0] == "M":
                        g = s[1]
                        wait_alone(sp, sp_passed, (m_free, i * GROUPS + g + 1))
                        for part in range(2):
                            sp.dma_start(stack[g % 2][96 + part:97 + part, 0, :, :].bitcast(F32)
                                         .rearrange("p h (r s) -> p (h r) s", s=P),
                                         m_stage[:, part, :].bitcast(F32)).then_inc(m_stacked[g % 2], 16)
                    elif s[0] == "OB":
                        wait_alone(sp, sp_passed, (o_free, START + i * TT + s[1] + 1))
                        sp.dma_start(x2_out[bass.ds(i * TT + s[1], 1)].rearrange("a p d -> p (a d)"),
                                     x_res[:, s[1], :]).then_inc(x2_stored, 16)
                if steps is LAST:
                    sp.wait_ge(x2_stored, START + 16 * TT * batches)

            staged_job = {}
            sp.sem_inc(x2_stored, START)
            in_loop(sp, program)

        @block.gpsimd
        def _(pool):
            consts = Tally(consts_ready)
            consts.inc(pool.memset(ident[:, :], 0.0))
            consts.inc(pool.memset(ident_bf[:, :], 0.0))
            consts.inc(pool.memset(masks[:, :, :], 0.0))
            consts.inc(pool.memset(ones[:, :], 1.0))
            consts.inc(pool.memset(maxima[:, :], 0.0))
            pool.wait_ge(consts_ready, consts.now())
            for m in (ident, ident_bf):
                consts.inc(pool.affine_select(out=m[:, :], in_=m[:, :], compare_op=ALU.not_equal, fill=1.0,
                                              base=0, pattern=[[-1, P]], channel_multiplier=1))
            consts.inc(pool.affine_select(out=masks[:, 2, :], in_=masks[:, 2, :], compare_op=ALU.is_ge, fill=MASKED,
                                          base=0, pattern=[[-(P + 1), P]], channel_multiplier=P))
            for m in range(2):
                consts.inc(pool.affine_select(out=masks[:, m, :], in_=masks[:, m, :], compare_op=ALU.is_ge,
                                              fill=MASKED, base=-1, pattern=[[-1, P]], channel_multiplier=1))
            for s in range(2):
                pool.wait_ge(consts_ready, consts.now())
                consts.inc(pool.memset(stack[s][96:98, KS, :, :].bitcast(F32), -1.0))
            pool.wait_ge(consts_ready, CONSTS)

            def select(view, first_block):
                count = view.shape[1] if len(view.shape) == 3 else None
                return pool.affine_select(out=view, in_=view, compare_op=ALU.is_ge, fill=0.0,
                                          base=0 if first_block else -1,
                                          pattern=([[0, count]] if count else []) + [[P if first_block else 1, P]],
                                          channel_multiplier=-(P + 1) if first_block else -1)

            def program(steps, i, first, parity):
                for s, n, _ in jobs(steps, first, parity):
                    if s[0] == "XRES":
                        pool.wait_ge(x_loaded, i * 16 + 16)
                        pool.wait_ge(mm_free, first)
                        pool.wait_ge(x2_stored, START + i * 16 * TT)
                        for j in range(TT):
                            pool.tensor_tensor(x_res[:, j, :], x_in[:, j, :], bias_sb[:, :], ALU.add
                                               ).then_inc(xres_ready, 1)
                    elif s[0] == "T":
                        k = s[2]
                        wait_alone(pool, pool_passed, (exp_done, i * TB + UNITS * s[1] + k + 1))
                        blocks = probs[:, k, :].rearrange("p (c x) -> p c x", x=P)
                        view = probs[:, k, 0:P] if k % 5 in (0, 2) else blocks[:, 0:4:3 if k % 5 < 4 else 2, :]
                        select(view, k % 5 in (0, 2)).then_inc(selected, 1)

            in_loop(pool, program)

        @block.tensor
        def _(pe):
            def split_product(out, a_hi, a_lo, b_hi, b_lo, tiles, part=None):
                pairs = [(a, b, k) for k in tiles for a, b in ((a_hi, b_hi), (a_hi, b_lo), (a_lo, b_hi))]
                third = len(pairs) // 3
                start, stop = (0, len(pairs)) if part is None else (part * third, part * third + third)
                for m, (a, b, k) in list(enumerate(pairs))[start:stop]:
                    last = pe.matmul(out, a(k), b(k), start=m == 0, stop=m == len(pairs) - 1)
                return last

            def s_unit(g, k, out):
                st = stack[g % 2]
                pair, u = divmod(k, 5)

                def block(h, r, t1, cols, start=True):
                    pe.matmul(out[:, cols:cols + t1], st[0:96, QS, h, P * r:P * r + P], st[0:96, KS, h, 0:t1],
                              start=start, stop=False, skip_group_check=True)

                def mask(view, added):
                    return pe.matmul(view, ident_bf[:, :], added, start=False, stop=True, skip_group_check=True)

                if u < 4 and u % 2 == 0:
                    block(2 * pair + u // 2, 3, 512, 0)
                    return mask(out[:, 384:512], masks[:, 0, :])
                if u < 4:
                    block(2 * pair + u // 2, 2, 384, 0)
                    block(2 * pair + u // 2, 0, 128, 384, start=False)
                    return mask(out[:, 256:512], masks[:, 1:3, :].rearrange("p m x -> p (m x)"))
                block(2 * pair, 1, 256, 0)
                block(2 * pair + 1, 1, 256, 256, start=False)
                return mask(out[:, :].rearrange("p (h t) -> p h t", h=2)[:, :, P:2 * P], masks[:, 0:2, :])

            def t_unit(g, k, out):
                st = stack[g % 2]
                pair, u = divmod(k, 5)

                def block(h, r, cols):
                    return pe.matmul(out[:, cols:cols + S - P * r], st[0:98, KS, h, P * r:P * r + P],
                                     st[0:98, QS, h, P * r:S], start=True, stop=True)

                if u < 4 and u % 2 == 0:
                    return block(2 * pair + u // 2, 0, 0)
                if u < 4:
                    block(2 * pair + u // 2, 1, 0)
                    return block(2 * pair + u // 2, 3, 384)
                block(2 * pair, 2, 0)
                return block(2 * pair + 1, 2, 256)

            def pv(g, r):
                for target in (o_bank, sum_bank):
                    for h in range(GH):
                        base = 5 * (h // 2)
                        unit, cols = {0: (base + 2 * (h % 2), 0), 1: (base + 2 * (h % 2) + 1, 0),
                                      3: (base + 2 * (h % 2) + 1, 384), 2: (base + 4, 256 * (h % 2))}[r]
                        weights = (v_sb[:, r, (GH * g + h) * HD:(GH * g + h + 1) * HD] if target is o_bank
                                   else ones[:, 0:HD])
                        last = pe.matmul(target[HD * h:HD * h + HD, P * r:S], weights,
                                         probs[:, unit, cols:cols + S - P * r], start=r == PV_ORDER[0],
                                         stop=r == PV_ORDER[-1])
                return last

            def out_part(j, groups):
                pairs = [(part, w, g) for g in groups for part, w in ((0, wT_hi), (0, wT_lo), (1, wT_hi))]
                for m, (part, w, g) in enumerate(pairs):
                    last = pe.matmul(out_bank[j][:, :], attn[g][part][:, P * j:P * j + P], w[:, 3, g, :],
                                     start=g == 0 and m == 0, stop=g == GROUPS - 1 and m == len(pairs) - 1)
                return last

            def program(steps, i, first, parity):
                for s, n, out in jobs(steps, first, parity):
                    b = batch_of(s, i)
                    part = None
                    if s[0] == "PART":
                        part, s = s[3], s[1:3]
                        begun[s] = True
                    elif begun.pop(s, False):
                        part = 2
                    banks = 4 if steps is SETUP else 2
                    if n is not None and part in (None, 0) and not (isinstance(n, int) and n < banks):
                        pe.wait_ge(mm_free, n + 1 - banks)
                    if s[0] == "W":
                        if s[2] == 0:
                            pe.wait_ge(w_loaded[s[1]], 16)
                            pe.wait_ge(consts_ready, CONSTS)
                        src = w_rows[s[1]]
                        for j in range(4):
                            last = pe.transpose(out[:, P * j:P * j + P], src[:, j, P * s[2]:P * s[2] + P], ident[:, :])
                        last.then_inc(mm_full, 1)
                    elif s[0] == "BIAS":
                        pe.wait_ge(mm_free, n)
                        pe.wait_ge(ot_ready, 1)
                        split_product(out[:, :], lambda k: attn_hi[:, 0, P * k:P * k + P],
                                      lambda k: attn_lo[:, 0, P * k:P * k + P],
                                      lambda k: wT_hi[:, 3, k, :], lambda k: wT_lo[:, 3, k, :], range(4))
                        pe.matmul(out[:, :], ones[0:1, :], o_recip[0:1, :], start=False, stop=True,
                                  skip_group_check=True).then_inc(mm_full, 1)
                    elif s[0] in ("XT", "CT"):
                        if s == ("XT", 0):
                            pe.wait_ge(xhat_ready, b * TT + TT)
                        elif s == ("CT", 0 if i is None else 2):
                            pe.wait_ge(c_loaded, b * 16 + 16)
                        src = first_context if s[0] == "CT" and i is None else xc_rows
                        for j in range(TT):
                            last = pe.transpose(out[:, P * j:P * j + P], src[:, j, P * s[1]:P * s[1] + P], ident[:, :])
                        last.then_inc(mm_full, 1)
                    elif s[0] in ("Q", "K"):
                        w, t_hi, t_lo = (0, xT_hi, xT_lo) if s[0] == "Q" else (1, cT_hi, cT_lo)
                        if s[1] == 0 and part in (None, 0):
                            pe.wait_ge(mm_free, transposed[s[0]] + 1 if i is not None else n)
                        g = s[1]
                        last = split_product(out[:, :], lambda k: wT_hi[:, w, k, P * g:P * g + P],
                                             lambda k: wT_lo[:, w, k, P * g:P * g + P],
                                             lambda k: t_hi[:, k, :], lambda k: t_lo[:, k, :], range(KT), part)
                        if part in (None, 2):
                            last.then_inc(mm_full, 1)
                    elif s[0] == "V":
                        j = s[1]
                        last = split_product(out[:, :], lambda k: cT_hi[:, k, P * j:P * j + P],
                                             lambda k: cT_lo[:, k, P * j:P * j + P],
                                             lambda k: wT_hi[:, 2, k, :], lambda k: wT_lo[:, 2, k, :], range(KT), part)
                        if part in (None, 2):
                            last.then_inc(mm_full, 1)
                        v_job[s[1]] = n
                    elif s[0] == "S":
                        u = UNITS * s[1] + s[2]
                        if u == 0:
                            pe.wait_ge(o_free, START + i * TT)
                        if s[2] in (0, 5):
                            pe.wait_ge(qk_stacked[s[1] % 2][s[2] // 5], (i * 2 + s[1] // 2 + 1) * 96)
                        if s[2] == 0 and s[1] > 0:
                            pe.wait_ge(m_free, i * GROUPS + s[1])
                        if u >= 2:
                            pe.wait_ge(s_free, i * SB + u - 1)
                        s_unit(s[1], s[2], s_bank[u % 2]).then_inc(s_full, 1)
                    elif s[0] == "M":
                        pe.wait_ge(s_free, i * SB + UNITS * s[1] + UNITS)
                        pe.transpose(m_bank[:, 0:P], maxima[:, :], ident[:, :]).then_inc(m_full, 1)
                    elif s[0] == "T":
                        u = UNITS * s[1] + s[2]
                        if u == 0:
                            pe.wait_ge(o_free, START + i * TT)
                        if s[2] == 0:
                            pe.wait_ge(m_stacked[s[1] % 2], (i * 2 + s[1] // 2 + 1) * 32)
                        if u >= 2:
                            pe.wait_ge(exp_done, i * TB + u - 1)
                        t_unit(s[1], s[2], t_bank[u % 2]).then_inc(t_full, 1)
                    elif s[0] == "PV":
                        g, r = s[1:]
                        if r == PV_ORDER[0]:
                            pe.wait_ge(selected, i * TB + UNITS * g + UNITS)
                            if g > 0:
                                pe.wait_ge(o_copied, i * (GROUPS - 1) + g)
                            else:
                                pe.wait_ge(o_normed, i * NORMS + 1)
                        if g == 0:
                            pe.wait_ge(mm_free, v_job[r] + 1)
                        last = pv(g, r)
                        if r == PV_ORDER[-1]:
                            last.then_inc(pv_done, 1)
                    elif s[0] == "OA":
                        if s[1:] == (0, 0):
                            pe.wait_ge(ot_ready, i * NORMS + 3)
                            pe.wait_ge(m_free, i * GROUPS + GROUPS)
                        if s[1:] == (2, 0):
                            pe.wait_ge(exp_done, i * TB + TB)
                        out_part(s[1], (s[2],))
                    elif s[0] == "OC":
                        if s[1] == 0:
                            pe.wait_ge(ot_ready, i * NORMS + 4)
                        out_part(s[1], (2,))
                    elif s[0] == "OB":
                        pe.wait_ge(ot_ready, i * NORMS + 5 + s[1])
                        out_part(s[1], (3,)).then_inc(o_full, 1)
                    if s[0] in ("XT", "CT"):
                        transposed["Q" if s[0] == "XT" else "K"] = n

                if steps is SETUP:
                    pe.wait_ge(mm_free, MM0)

            transposed, begun, v_job = {}, {}, {}
            in_loop(pe, program)

        @block.scalar
        def _(act):
            def program(steps, i, first, parity):
                chain = Tally(act_self, 0 if i is None else i + 1)
                for s, n, out in jobs(steps, first, parity):
                    b = batch_of(s, i)
                    if s[0] == "M":
                        act.wait_ge(m_full, i * GROUPS + s[1] + 1)
                        act.activation(m_stage[:, 0, :], m_bank[0:16, 0:P], ACT.Copy).then_inc(m_hi, 1)
                    elif s[0] in ("W", "XT", "CT", "Q", "K"):
                        act.wait_ge(mm_full, n + 1)
                        if s[0] == "W":
                            dst = wT_hi[:, s[1], s[2], :]
                        elif s[0] == "XT":
                            dst = xT_hi[:, s[1], :]
                        elif s[0] == "CT":
                            dst = cT_hi[:, s[1], :]
                        else:
                            dst = stage[:, 0 if s[0] == "Q" else 2, :]
                            for p in range(2):
                                staged(act, [q[p] for q in qk_stacked], s[1], b, 96)
                        act.activation(dst, out[:, :], ACT.Copy).then_inc(mm_hi, 1)
                    elif s[0] == "BV":
                        act.wait_ge(o_normed, 1)
                        act.activation(attn_hi[:, 0, :], o_norm[:, :], ACT.Copy).then_inc(ot_hi, 1)
                    elif s[0] == "BIAS":
                        act.wait_ge(mm_full, n + 1)
                        act.activation(bias_sb[:, :], out[:, :], ACT.Copy).then_inc(mm_hi, 1)
                    elif s[0] == "LN_VAR":
                        act.wait_ge(var_ready, b + 1)
                        ln_rstd(act, chain, ln).then_inc(rstd_ready, 1)
                    elif s[0] == "T":
                        u = UNITS * s[1] + s[2]
                        act.wait_ge(t_full, i * TB + u + 1)
                        act.activation(probs[:, s[2], :], t_bank[u % 2][:, :], ACT.Exp, scale=SCALE
                                       ).then_inc(exp_done, 1)
                    elif s[0] == "NC":
                        g = s[1]
                        act.wait_ge(pv_done, i * GROUPS + g + 1)
                        act.wait_ge(ot_ready, i * NORMS + g + 1)
                        act.activation(o_recip[:, :], sum_bank[:, :], ACT.Copy)
                        act.activation(o_norm[:, :], o_bank[:, :], ACT.Copy).then_inc(o_copied, 1)
                    elif s[0] == "NH" and s[1] == GROUPS - 1:
                        cols, number = norm_part(*s[1:])
                        act.wait_ge(o_normed, i * NORMS + number + 2)
                        act.activation(attn[s[1]][0][:, cols], o_norm[:, cols], ACT.Copy).then_inc(ot_hi, 1)

            in_loop(act, program)

        @block.vector
        def _(dve):
            def program(steps, i, first, parity):
                chain = Tally(dve_self, 0 if i is None else i * CHAIN + CHAIN0)
                hi = 0 if i is None else i * (MMB - HI_SKIP) + MM0
                highs = 0
                for s, n, out in jobs(low_parts_later(steps), first, parity):
                    b = batch_of(s, i)
                    if s[0] == "M":
                        dve.wait_ge(m_hi, i * GROUPS + s[1] + 1)
                        dve.tensor_tensor(m_stage[:, 1, :], m_bank[0:16, 0:P], m_stage[:, 0, :].bitcast(F32),
                                          ALU.subtract).then_inc(m_free, 1)
                    elif s[0] in ("W", "XT", "CT", "Q", "K"):
                        a_hi, a_lo = {"W": lambda: (wT_hi[:, s[1], s[2], :], wT_lo[:, s[1], s[2], :]),
                                  "XT": lambda: (xT_hi[:, s[1], :], xT_lo[:, s[1], :]),
                                  "CT": lambda: (cT_hi[:, s[1], :], cT_lo[:, s[1], :]),
                                  "Q": lambda: (stage[:, 0, :], stage[:, 1, :]),
                                  "K": lambda: (stage[:, 2, :], stage[:, 3, :])}[s[0]]()
                        highs += 1
                        dve.wait_ge(mm_hi, hi + highs)
                        dve.tensor_tensor(a_lo, out[:, :], a_hi.bitcast(F32), ALU.subtract
                                          ).then_inc(mm_free, 1)
                    elif s[0] == "BV":
                        dve.wait_ge(b_loaded, 32)
                        dve.wait_ge(consts_ready, CONSTS)
                        for g in range(GROUPS):
                            last = dve.tensor_scalar(o_norm[:, P * g:P * g + P], ones[:, :], bv_col[:, g:g + 1], None,
                                                     ALU.mult)
                        last.then_inc(o_normed, 1)
                        dve.wait_ge(ot_hi, 1)
                        dve.tensor_tensor(attn_lo[:, 0, :], o_norm[:, :], attn_hi[:, 0, :].bitcast(F32), ALU.subtract
                                          ).then_inc(ot_ready, 1)
                    elif s[0] == "BIAS":
                        highs += 1
                        dve.wait_ge(mm_hi, hi + highs)
                        dve.tensor_copy(o_norm[:, :], bias_sb[:, :]).then_inc(mm_free, 1)
                    elif s[0] == "V":
                        dve.wait_ge(mm_full, n + 1)
                        dve.tensor_copy(v_sb[:, s[1], :], out[:, :]).then_inc(mm_free, 1)
                    elif s[0] == "S":
                        u = UNITS * s[1] + s[2]
                        bank_u = s_bank[u % 2]
                        pair, k = divmod(s[2], 5)
                        dve.wait_ge(s_full, i * SB + u + 1)
                        if k < 4 and k % 2 == 0:
                            col = 4 * (2 * pair + k // 2)
                            last = dve.tensor_reduce(maxima[:, col + 3:col + 4], bank_u[:, :], AX.X, ALU.max)
                        elif k < 4:
                            col = 4 * (2 * pair + k // 2)
                            dve.tensor_reduce(maxima[:, col + 2:col + 3], bank_u[:, 0:384], AX.X, ALU.max)
                            last = dve.tensor_reduce(maxima[:, col:col + 1], bank_u[:, 384:512], AX.X, ALU.max)
                        else:
                            col = 8 * pair + 1
                            last = dve.tensor_reduce(maxima[:, col:col + 5:4],
                                                     bank_u[:, :].rearrange("p (h t) -> p h t", h=2), AX.X, ALU.max)
                        last.then_inc(s_free, 1)
                    elif s[0] == "LN_STATS":
                        if s[1] == 0:
                            dve.wait_ge(x_loaded, b * 16 + 16)
                        ln_stats(dve, chain, ln, x_in, s[1])
                    elif s[0] == "LN_VAR":
                        ln_var(dve, chain, ln, TT, dve_passed).then_inc(var_ready, 1)
                    elif s[0] == "LN_RSTD":
                        dve.wait_ge(rstd_ready, b + 1)
                        ln_newton(dve, chain, ln)
                    elif s[0] == "LN_APPLY":
                        ln_apply(dve, ln, x_in, xc_rows, s[1], xhat_ready)
                    elif s[0] == "NR":
                        g, c = s[1:]
                        if c == 0 and g < GROUPS - 1:
                            dve.wait_ge(o_copied, i * (GROUPS - 1) + g + 1)
                        elif c == 0:
                            dve.wait_ge(pv_done, i * GROUPS + g + 1)
                        src = sum_bank if g == GROUPS - 1 else o_recip
                        chain.inc(dve.reciprocal(o_recip[:, P * c:P * c + P], src[:, P * c:P * c + P]))
                    elif s[0] == "NM":
                        cols, _number = norm_part(*s[1:])
                        dve.wait_ge(dve_self, chain.now())
                        src = o_bank if s[1] == GROUPS - 1 else o_norm
                        dve.tensor_tensor(o_norm[:, cols], src[:, cols], o_recip[:, cols], ALU.mult
                                          ).then_inc(o_normed, 1)
                    elif s[0] == "NH" and s[1] < GROUPS - 1:
                        number = norm_part(*s[1:])[1]
                        dve.wait_ge(o_normed, i * NORMS + number + 2)
                        dve.tensor_copy(attn[s[1]][0], o_norm[:, :]).then_inc(ot_hi, 1)
                    elif s[0] == "NL":
                        cols, number = norm_part(*s[1:])
                        hi_part, lo_part = attn[s[1]]
                        dve.wait_ge(ot_hi, i * NORMS + number + 2)
                        dve.tensor_tensor(lo_part[:, cols], o_norm[:, cols], hi_part[:, cols].bitcast(F32),
                                          ALU.subtract).then_inc(ot_ready, 1)
                    elif s[0] == "OB":
                        j = s[1]
                        dve.wait_ge(o_full, i * TT + j + 1)
                        if j == 0:
                            dve.wait_ge(xres_ready, i * TT + TT)
                        dve.tensor_tensor(x_res[:, j, :], out_bank[j][:, :], x_res[:, j, :], ALU.add
                                          ).then_inc(o_free, 1)
                if steps is SETUP:
                    assert chain.local == CHAIN0
                elif steps is STEADY:
                    assert chain.local == CHAIN

            dve.sem_inc(o_free, START)
            in_loop(dve, program)


HIDDEN_LAG = 4


def ffn_steps(blocks, more):
    layernorm = {4: [("LN_STATS", 0)], 5: [("LN_STATS", 1)], 6: [("LN_STATS", 2)], 7: [("LN_STATS", 3), ("LN_VAR",)],
                 9: [("LN_RSTD",)], 11: [("LN_NEWTON",), ("LN_APPLY", 0), ("LN_APPLY", 1)],
                 12: [("LN_APPLY", 2), ("LN_APPLY", 3)]}
    steps = [("COPY",)]
    for b in range(blocks):
        steps.append(("H", b))
        if b >= HIDDEN_LAG:
            steps.append(("Y", b - HIDDEN_LAG))
        if more:
            steps += layernorm.get(b, [])
    for m, b in enumerate(range(blocks - HIDDEN_LAG, blocks)):
        if more:
            steps.append(("XT", m))
        steps.append(("Y", b))
    steps += [("RES", j) for j in range(4)]
    if more:
        steps.insert(len(steps) - 4, ("Z",))
    return steps


def ffn_phase(nc, dram, batches):
    x2_in, fast_b, w_fc, w_proj, u_in, v_in, gate, y_out = dram
    HIDDEN, D = w_fc.shape
    RANK = u_in.shape[1]
    KT, NB, TT, OT = D // P, HIDDEN // P, 4, D // P
    S = TT * P
    CHUNKS = HIDDEN // D
    assert RANK <= 32 and D == 512 and KT == 4 and HIDDEN_LAG == KT
    STEADY, LAST = ffn_steps(NB, True), ffn_steps(NB, False)
    XJ = KT + 1
    RING = 8

    with ExitStack() as c:
        def sb(name, shape, dt=F32):
            return c.enter_context(nc.sbuf_tensor(name, shape, dt))

        def sem(name):
            return c.enter_context(nc.semaphore(name))

        fcT = sb("fcT", [P, KT, HIDDEN], F32R)
        projT = sb("projT", [P, NB, D], F32R)
        a_stack = sb("a_stack", [P, KT, P], F32R)
        u_stack = sb("u_stack", [P, HIDDEN], F32R)
        w_nat = sb("w_nat", [P, 4, D])
        tern = sb("tern", [P, 2, D], BF16)
        neg = sb("neg", [P, 2, D], BF16)
        u_nat = sb("u_nat", [P, NB, RANK])
        u_hi = sb("u_hi", [P, NB, RANK], F32R)
        u_lo = sb("u_lo", [P, NB, RANK], F32R)
        u_cols = sb("u_cols", [P, NB, P])
        v_sb = sb("v_rows", [RANK, D])
        fb_sb = sb("fb_sb", [RANK, RANK])
        fbT = sb("fbT", [RANK, RANK])
        gate_sb = sb("gate_sb", [1, 1])
        gate_col = sb("gate_col", [P, 1])
        a_f32 = sb("a_f32", [P, KT, RANK])
        scale_fc = sb("scale_fc", [P, NB])
        scale_pr = sb("scale_pr", [P, OT])
        parts = sb("parts", [P, NB + OT * CHUNKS])
        half = sb("half", [P, NB + OT])
        neg_half = sb("neg_half", [P, NB + OT])
        inv_fc = sb("inv_fc", [P, NB])
        diag = sb("diag", [P, OT, P])
        scale_row = sb("scale_row", [P, D])
        ident = sb("ident2", [P, P])
        ident_bf = sb("ident2_bf", [P, P], BF16)
        ones = sb("ones2", [P, P])
        xT_hi = sb("x2T_hi", [P, KT, S], F32R)
        xT_lo = sb("x2T_lo", [P, KT, S], F32R)
        x_in = sb("x2_in_sb", [P, TT, D])
        x_res = sb("x2_res", [P, TT, D])
        x_hat = sb("x2_hat", [P, TT, D])
        y_sb = sb("y_sb", [P, TT, D])
        z_sb = sb("z_sb", [P, S], F32R)
        relu = sb("relu", [P, 2, S])
        act_sq = sb("act_sq", [P, 2, S])
        a_hi = sb("a_hi", [P, RING, S], F32R)
        a_lo = sb("a_lo", [P, RING, S], F32R)
        ln = layernorm_buffers(lambda n, s: sb(f"{n}2", s), TT)

        h_bank = [c.enter_context(nc.psum_tensor(f"h_bank{n}", [P, 512], F32)) for n in range(2)]
        x_bank = [c.enter_context(nc.psum_tensor(f"x_bank{n}", [P, 512], F32)) for n in range(2)]
        y_bank = [c.enter_context(nc.psum_tensor(f"y_bank{n}", [P, 512], F32)) for n in range(4)]

        wn_loaded = [sem(f"wn_loaded{n}") for n in range(3)]
        small_loaded = sem("small_loaded")
        consts_ready = sem("consts2_ready")
        sums_ready = sem("sums_ready")
        tern_ready = sem("tern_ready")
        tern_full = sem("tern_full")
        tern_out = sem("tern_out")
        prep = sem("prep")
        x2_loaded = sem("x2_loaded")
        h_full = sem("h_full")
        relu_done = sem("relu_done")
        sq_done = sem("sq_done")
        hid_hi = sem("hid_hi")
        hid_ready = sem("hid_ready")
        y_full = sem("y_full")
        y_free = sem("y_free")
        y_ready = sem("y_ready")
        y_stored = sem("y_stored")
        xm_full = sem("xm_full")
        xm_hi = sem("xm_hi")
        xm_free = sem("xm_free")
        var_ready = sem("var2_ready")
        rstd_ready = sem("rstd2_ready")
        act_self = sem("act2_self")
        dve_self = sem("dve2_self")
        xhat_ready = sem("xhat2_ready")
        xres_ready = sem("xres2_ready")
        sp_passed, pool_passed, dve_passed = sem("sp2_passed"), sem("pool2_passed"), sem("dve2_passed")

        PIECES = [("fc", t, 0) for t in range(NB)] + [("pr", t, q) for t in range(OT) for q in range(CHUNKS)]
        w_rows = (w_nat, y_sb, x_res)
        SUMS_AHEAD = 6
        (PREP_GATE_PE, PREP_GATE_ACT, PREP_A_PE, PREP_A_DVE, PREP_A_HIGH_ACT, PREP_A_LOW_DVE, PREP_U_DVE,
         PREP_U_HIGH_ACT, PREP_U_COLS_DVE, PREP_U_PE, PREP_U_ACT, PREP_SCALE_DVE, PREP_SCALE_PE,
         PREP_SCALE_ACT) = range(1, 15)

        X_BEHIND = {3: (2, 3), 11: (KT,)}
        U_COLS_BEHIND = NB + 3

        def piece_rows(q):
            return w_rows[q // 4 % 3][:, q % 4, :]

        CONSTS = 7
        CHAIN0 = CHAIN = 12

        block = c.enter_context(nc.Block())

        def in_loop(engine, program):
            if batches > 1:
                with engine.Fori(0, batches - 1, 1) as i:
                    program(STEADY, i)
            program(LAST, batches - 1)

        @block.sync
        def _(sp):
            sp.dma_start(x_in[:, :, :], x2_in[0:TT].rearrange("j p d -> p j d")).then_inc(x2_loaded, 16)
            for load in range(len(PIECES) // 4):
                if load >= 3:
                    sp.wait_ge(tern_ready, 4 * (load - 2))
                src = (w_fc[4 * P * load:4 * P * load + 4 * P].rearrange("(j p) d -> p j d", p=P) if load < NB // 4
                       else w_proj[P * (load - NB // 4):P * (load - NB // 4) + P].rearrange("p (j d) -> p j d", d=D))
                sp.dma_start(w_rows[load % 3][:, :, :], src).then_inc(wn_loaded[load % 3], 16)
                if load == 0:
                    with nc.allow_non_contiguous_dma(reason="rows of 16 values, once"):
                        sp.dma_start(u_nat[:, :, :], u_in.rearrange("(b p) r -> p b r", p=P)).then_inc(small_loaded, 16)
                        sp.dma_start(v_sb[:, :], v_in).then_inc(small_loaded, 16)
                        sp.dma_start(fb_sb[:, :], fast_b).then_inc(small_loaded, 16)
                        sp.dma_start(gate_sb[:, :], gate).then_inc(small_loaded, 16)

            def program(steps, i):
                for s in steps:
                    if s[0] == "COPY" and steps is STEADY:
                        wait_alone(sp, sp_passed, (xres_ready, i * TT + TT))
                        wait_alone(sp, sp_passed, (xm_free, i * XJ + XJ))
                        sp.dma_start(x_in[:, :, :], x2_in[bass.ds(i * TT + TT, TT)].rearrange("j p d -> p j d")
                                     ).then_inc(x2_loaded, 16)
                    elif s[0] == "RES":
                        wait_alone(sp, sp_passed, (y_ready, START + i * TT + s[1] + 1))
                        sp.dma_start(y_out[bass.ds(i * TT + s[1], 1)].rearrange("a p d -> p (a d)"), y_sb[:, s[1], :]
                                     ).then_inc(y_stored, 16)

            sp.sem_inc(y_stored, START)
            in_loop(sp, program)
            sp.wait_ge(y_stored, START + 16 * TT * batches)

        @block.gpsimd
        def _(pool):
            consts = Tally(consts_ready)
            consts.inc(pool.memset(ident[:, :], 0.0))
            consts.inc(pool.memset(ident_bf[:, :], 0.0))
            consts.inc(pool.memset(ones[:, :], 1.0))
            consts.inc(pool.memset(u_cols[:, :, :], 0.0))
            consts.inc(pool.memset(a_stack[:, :, :].bitcast(F32), 0.0))
            pool.wait_ge(consts_ready, consts.now())
            for m in (ident, ident_bf):
                consts.inc(pool.affine_select(out=m[:, :], in_=m[:, :], compare_op=ALU.not_equal, fill=1.0,
                                              base=0, pattern=[[-1, P]], channel_multiplier=1))

            def program(steps, i):
                for s in steps:
                    if s[0] == "COPY":
                        wait_alone(pool, pool_passed, (x2_loaded, i * 16 + 16), (y_ready, START + i * TT))
                        for j in range(TT):
                            pool.tensor_copy(x_res[:, j, :], x_in[:, j, :]).then_inc(xres_ready, 1)

            wait_alone(pool, pool_passed, (tern_ready, len(PIECES)))
            in_loop(pool, program)

        @block.tensor
        def _(pe):
            def transposed(target, src, k):
                for j in range(TT):
                    last = pe.transpose(target[:, P * j:P * j + P], src[:, j, P * k:P * k + P], ident[:, :])
                return last

            def tern_transposes(q):
                pe.wait_ge(tern_ready, q + 1)
                if q >= 2:
                    pe.wait_ge(tern_out, q - 1)
                out = h_bank[q % 2][:, 0:256].bitcast(BF16)
                for k in range(4):
                    last = pe.transpose(out[:, P * k:P * k + P], tern[:, q % 2, P * k:P * k + P], ident_bf[:, :])
                last.then_inc(tern_full, 1)

            def z_product(n):
                pe.wait_ge(xm_free, n)
                for k in range(KT):
                    for part in (xT_hi, xT_lo):
                        last = pe.matmul(x_bank[0][:, :], a_stack[:, k, :], part[:, k, :],
                                         start=k == 0 and part is xT_hi, stop=k == KT - 1 and part is xT_lo)
                last.then_inc(xm_full, 1)

            pe.wait_ge(consts_ready, CONSTS)
            pe.wait_ge(small_loaded, 64)
            pe.matmul(x_bank[0][0:RANK, 0:RANK], fb_sb[:, :], ident[0:RANK, 0:RANK], start=True, stop=True)
            pe.matmul(x_bank[0][:, 32:33], ones[0:1, :], gate_sb[:, :], start=True, stop=True).then_inc(prep, 1)
            pe.wait_ge(prep, PREP_GATE_ACT)
            for k in range(KT):
                last = pe.matmul(x_bank[1][:, RANK * k:RANK * k + RANK], v_sb[:, P * k:P * k + P], fbT[:, :],
                                 start=True, stop=True)
            last.then_inc(prep, 1)
            pe.wait_ge(prep, PREP_A_DVE)
            pe.wait_ge(xhat_ready, TT)
            for k in range(2):
                transposed(x_bank[k % 2], x_hat, k).then_inc(xm_full, 1)
            for q in range(len(PIECES)):
                tern_transposes(q)
                for k in X_BEHIND.get(q, ()):
                    if k < KT:
                        pe.wait_ge(xm_free, k - 1)
                        transposed(x_bank[k % 2], x_hat, k).then_inc(xm_full, 1)
                    else:
                        pe.wait_ge(prep, PREP_A_LOW_DVE)
                        z_product(KT)
                if q == U_COLS_BEHIND:
                    pe.wait_ge(prep, PREP_U_COLS_DVE)
                    for b in range(NB):
                        last = pe.transpose(y_bank[b // 4][:, P * (b % 4):P * (b % 4) + P], u_cols[:, b, :], ident[:, :])
                    last.then_inc(prep, 1)
            pe.wait_ge(prep, PREP_SCALE_DVE)
            pe.wait_ge(xm_free, KT + 1)
            for j in range(OT):
                last = pe.matmul(x_bank[0][:, P * j:P * j + P], ones[:, :], diag[:, j, :], start=True, stop=True)
            last.then_inc(prep, 1)
            pe.wait_ge(prep, PREP_SCALE_ACT)
            pe.wait_ge(tern_out, len(PIECES))

            def program(steps, i):
                for s in steps:
                    if s[0] == "H":
                        b = s[1]
                        if b >= 2:
                            pe.wait_ge(relu_done, i * NB + b - 1)
                        cols = slice(P * b, P * b + P)
                        for k in range(KT):
                            pe.matmul(h_bank[b % 2][:, :], fcT[:, k, cols], xT_hi[:, k, :], start=k == 0, stop=False)
                            pe.matmul(h_bank[b % 2][:, :], fcT[:, k, cols], xT_lo[:, k, :], start=False, stop=False)
                        if b == 0:
                            pe.wait_ge(xm_free, i * XJ + XJ)
                        pe.matmul(h_bank[b % 2][:, :], u_stack[:, cols], z_sb[:, :], start=False, stop=True
                                  ).then_inc(h_full, 1)
                    elif s[0] == "Y":
                        b = s[1]
                        pe.wait_ge(hid_ready, i * NB + b + 1)
                        if b == 0:
                            pe.wait_ge(y_free, START + i * TT)
                        for j in range(TT):
                            pe.matmul(y_bank[j][:, :], a_hi[:, b % RING, P * j:P * j + P], projT[:, b, :],
                                      start=b == 0, stop=False)
                            last = pe.matmul(y_bank[j][:, :], a_lo[:, b % RING, P * j:P * j + P], projT[:, b, :],
                                             start=False, stop=b == NB - 1)
                        last.then_inc(y_full, 1)
                    elif s[0] == "XT":
                        k = s[1]
                        n = i * XJ + XJ + k
                        if k == 0:
                            pe.wait_ge(xhat_ready, i * TT + 2 * TT)
                        pe.wait_ge(xm_free, n if k == 0 else n - 1)
                        transposed(x_bank[k % 2], x_hat, k).then_inc(xm_full, 1)
                    elif s[0] == "Z":
                        z_product(i * XJ + XJ + KT)

            in_loop(pe, program)

        @block.scalar
        def _(act):
            def row_sum(q):
                if q % 4 == 0:
                    act.wait_ge(wn_loaded[q // 4 % 3], q // 12 * 16 + 16)
                if q >= 2:
                    act.wait_ge(sums_ready, q - 1)
                act.activation(relu[:, q % 2, :], piece_rows(q), ACT.Abs, accum_out=parts[:, q:q + 1]
                               ).then_inc(sums_ready, 1)

            def tern_copy(q):
                kind, t, piece = PIECES[q]
                act.wait_ge(tern_full, q + 1)
                src = h_bank[q % 2][:, 0:256].bitcast(BF16).rearrange("p (k c) -> p k c", k=4)
                dst = fcT[:, :, P * t:P * t + P] if kind == "fc" else projT[:, 4 * piece:4 * piece + 4,
                                                                          P * t:P * t + P]
                act.activation(dst, src, ACT.Copy).then_inc(tern_out, 1)

            def x_high(k, n):
                act.wait_ge(xm_full, n + 1)
                dst = xT_hi[:, k, :] if k < KT else z_sb[:, :]
                act.activation(dst, x_bank[k % 2][:, :], ACT.Copy).then_inc(xm_hi, 1)

            act.wait_ge(prep, PREP_GATE_PE)
            act.activation(fbT[:, :], x_bank[0][0:RANK, 0:RANK], ACT.Copy)
            act.activation(gate_col[:, :], x_bank[0][:, 32:33], ACT.Copy).then_inc(prep, 1)
            act.wait_ge(var_ready, 1)
            chain = Tally(act_self)
            ln_rstd(act, chain, ln).then_inc(rstd_ready, 1)
            for q in range(4):
                row_sum(q)
            act.wait_ge(prep, PREP_A_DVE)
            for col in (0, 32, 64):
                last = act.activation(a_stack[:, :, col:col + RANK], a_f32[:, :, :], ACT.Copy)
            last.then_inc(prep, 1)
            for k in range(2):
                x_high(k, k)
            for q in range(4, SUMS_AHEAD):
                row_sum(q)
            for q in range(len(PIECES)):
                if q + SUMS_AHEAD < len(PIECES):
                    row_sum(q + SUMS_AHEAD)
                tern_copy(q)
                for k in X_BEHIND.get(q, ()):
                    x_high(k, k)
                if q == NB - 1:
                    act.wait_ge(prep, PREP_U_DVE)
                    act.activation(u_hi[:, :, :], u_nat[:, :, :], ACT.Copy).then_inc(prep, 1)
                if q == U_COLS_BEHIND + 4:
                    act.wait_ge(prep, PREP_U_PE)
                    for m in range(4):
                        last = act.activation(u_stack[:, 512 * m:512 * m + 512], y_bank[m][:, :], ACT.Copy)
                    last.then_inc(prep, 1)
            act.wait_ge(prep, PREP_SCALE_PE)
            act.activation(scale_row[:, :], x_bank[0][:, :], ACT.Copy).then_inc(prep, 1)

            def program(steps, i):
                chain = Tally(act_self, i + 1)
                for s in steps:
                    if s[0] == "H":
                        b = s[1]
                        act.wait_ge(h_full, i * NB + b + 1)
                        act.activation(relu[:, b % 2, :], h_bank[b % 2][:, :], ACT.Relu, scale=scale_fc[:, b:b + 1]
                                       ).then_inc(relu_done, 1)
                        act.wait_ge(relu_done, i * NB + b + 1)
                        if b >= 2:
                            act.wait_ge(hid_ready, i * NB + b - 1)
                        act.activation(act_sq[:, b % 2, :], relu[:, b % 2, :], ACT.Square).then_inc(sq_done, 1)
                    elif s[0] == "LN_RSTD":
                        act.wait_ge(var_ready, i + 2)
                        ln_rstd(act, chain, ln).then_inc(rstd_ready, 1)
                    elif s[0] in ("XT", "Z"):
                        k = s[1] if s[0] == "XT" else KT
                        x_high(k, i * XJ + XJ + k)

            in_loop(act, program)

        @block.vector
        def _(dve):
            self_ = Tally(dve_self)

            def step(instruction):
                self_.inc(instruction)
                dve.wait_ge(dve_self, self_.now())

            def thresholds(load):
                dve.wait_ge(sums_ready, 4 * load + 4)
                total, length = parts[:, 4 * load:4 * load + 4], D
                if load < NB // 4:
                    cols, scale = slice(4 * load, 4 * load + 4), scale_fc[:, 4 * load:4 * load + 4]
                else:
                    t = load - NB // 4
                    cols, scale, length = slice(NB + t, NB + t + 1), scale_pr[:, t:t + 1], HIDDEN
                    step(dve.tensor_reduce(scale, total, AX.X, ALU.add))
                    total = scale
                step(dve.tensor_scalar(scale, total, 1.0 / length, 1e-5, ALU.mult, ALU.max))
                self_.inc(dve.tensor_scalar(half[:, cols], scale, 0.5, None, ALU.mult))
                step(dve.tensor_scalar(neg_half[:, cols], scale, -0.5, None, ALU.mult))

            def ternary(pair):
                for q in pair:
                    col = q if q < NB else NB + (q - NB) // CHUNKS
                    if q >= 2:
                        dve.wait_ge(tern_ready, q - 1)
                    self_.inc(dve.tensor_scalar(neg[:, q % 2, :], piece_rows(q), neg_half[:, col:col + 1], None,
                                                ALU.is_lt))
                dve.wait_ge(dve_self, self_.now())
                for q in pair:
                    col = q if q < NB else NB + (q - NB) // CHUNKS
                    if q >= 2:
                        dve.wait_ge(tern_full, q - 1)
                    dve.scalar_tensor_tensor(tern[:, q % 2, :], piece_rows(q), half[:, col:col + 1], neg[:, q % 2, :],
                                             ALU.is_gt, ALU.subtract).then_inc(tern_ready, 1)

            def x_low(k, n):
                dve.wait_ge(xm_hi, n + 1)
                if k < KT:
                    dve.tensor_tensor(xT_lo[:, k, :], x_bank[k % 2][:, :], xT_hi[:, k, :].bitcast(F32), ALU.subtract
                                      ).then_inc(xm_free, 1)
                else:
                    dve.tensor_tensor(z_sb[32:64, :], x_bank[0][32:64, :], z_sb[32:64, :].bitcast(F32), ALU.subtract
                                      ).then_inc(xm_free, 1)

            dve.wait_ge(x2_loaded, 16)
            for j in range(TT):
                ln_stats(dve, self_, ln, x_in, j)
            ln_var(dve, self_, ln, TT, dve_passed).then_inc(var_ready, 1)
            dve.wait_ge(prep, PREP_A_PE)
            dve.tensor_scalar(a_f32[:, :, :].rearrange("p k r -> p (k r)"), x_bank[1][:, 0:KT * RANK],
                              gate_col[:, 0:1], None, ALU.mult).then_inc(prep, 1)
            dve.wait_ge(rstd_ready, 1)
            ln_newton(dve, self_, ln)
            for j in range(TT):
                ln_apply(dve, ln, x_in, x_hat, j, xhat_ready)
            dve.wait_ge(prep, PREP_A_HIGH_ACT)
            dve.wait_ge(consts_ready, CONSTS)
            dve.tensor_tensor(a_stack[:, :, 96:96 + RANK], a_f32[:, :, :], a_stack[:, :, 0:RANK].bitcast(F32),
                              ALU.subtract).then_inc(prep, 1)
            for load in range(len(PIECES) // 4):
                thresholds(load)
                ternary((4 * load, 4 * load + 1))
                ternary((4 * load + 2, 4 * load + 3))
                for k in X_BEHIND.get(4 * load - 1, ()) if load > 0 else (0, 1):
                    x_low(k, k)
                if load == NB // 4 - 1:
                    step(dve.reciprocal(inv_fc[:, :], scale_fc[:, :]))
                    for b in range(NB):
                        last = dve.tensor_scalar(u_nat[:, b, :], u_nat[:, b, :], inv_fc[:, b:b + 1], None, ALU.mult)
                    last.then_inc(prep, 1)
                if load == NB // 4:
                    dve.wait_ge(prep, PREP_U_HIGH_ACT)
                    step(dve.tensor_tensor(u_lo[:, :, :], u_nat[:, :, :], u_hi[:, :, :].bitcast(F32), ALU.subtract))
                    for col, src in ((0, u_hi), (32, u_hi), (64, u_lo), (96, u_hi)):
                        last = dve.tensor_copy(u_cols[:, :, col:col + RANK], src[:, :, :].bitcast(F32))
                    last.then_inc(prep, 1)
            dve.wait_ge(prep, PREP_U_ACT)
            for j in range(OT):
                last = dve.tensor_scalar(diag[:, j, :], ident[:, :], scale_pr[:, j:j + 1], None, ALU.mult)
            last.then_inc(prep, 1)
            setup = self_.now() - CHAIN0

            def program(steps, i):
                chain = Tally(dve_self, i * CHAIN + setup + CHAIN0)
                for s in steps:
                    if s[0] == "H":
                        b = s[1]
                        dve.wait_ge(sq_done, i * NB + b + 1)
                        if b >= RING:
                            dve.wait_ge(y_full, i * NB + b + 1 - RING)
                        dve.tensor_copy(a_hi[:, b % RING, :], act_sq[:, b % 2, :]).then_inc(hid_hi, 1)
                        dve.wait_ge(hid_hi, i * NB + b + 1)
                        dve.tensor_tensor(a_lo[:, b % RING, :], act_sq[:, b % 2, :], a_hi[:, b % RING, :].bitcast(F32),
                                          ALU.subtract).then_inc(hid_ready, 1)
                    elif s[0] == "LN_STATS":
                        if s[1] == 0:
                            dve.wait_ge(x2_loaded, i * 16 + 32)
                        ln_stats(dve, chain, ln, x_in, s[1])
                    elif s[0] == "LN_VAR":
                        ln_var(dve, chain, ln, TT, dve_passed).then_inc(var_ready, 1)
                    elif s[0] == "LN_NEWTON":
                        dve.wait_ge(rstd_ready, i + 2)
                        ln_newton(dve, chain, ln)
                    elif s[0] == "LN_APPLY":
                        ln_apply(dve, ln, x_in, x_hat, s[1], xhat_ready)
                    elif s[0] in ("XT", "Z"):
                        k = s[1] if s[0] == "XT" else KT
                        x_low(k, i * XJ + XJ + k)
                    elif s[0] == "RES":
                        j = s[1]
                        if j == 0:
                            dve.wait_ge(y_full, i * NB + NB)
                            dve.wait_ge(y_stored, START + i * 16 * TT)
                            dve.wait_ge(xres_ready, i * TT + TT)
                        dve.tensor_tensor(y_sb[:, j, :], y_bank[j][:, :], scale_row[:, :], ALU.mult
                                          ).then_inc(y_free, 1)
                        dve.wait_ge(y_free, START + i * TT + j + 1)
                        dve.tensor_tensor(y_sb[:, j, :], y_sb[:, j, :], x_res[:, j, :], ALU.add).then_inc(y_ready, 1)
                if steps is STEADY:
                    assert chain.local == CHAIN

            dve.sem_inc(y_free, START)
            dve.sem_inc(y_ready, START)
            in_loop(dve, program)


def xattn_ffn_kernel(nc, x, ctx_1024, Wq, Wk, Wv, bv, Wo, bo, fast_b, w_fc, w_proj, u, v, gate, out):
    batches = x.shape[0]
    tiles = batches * x.shape[1] // P
    x2 = nc.dram_tensor("x2", [tiles, P, x.shape[2]], F32, kind="Internal").ap()
    attention_phase(nc, (x, ctx_1024, Wq, Wk, Wv, bv, Wo, bo, x2), batches)
    ffn_phase(nc, (x2, fast_b, w_fc, w_proj, u, v, gate, out.rearrange("b (j p) d -> (b j) p d", p=P)), batches)


_INS = ["x", "ctx_1024", "L0_xattn_Wq", "L0_xattn_Wk", "L0_xattn_Wv", "L0_xattn_bv", "L0_xattn_Wo", "L0_xattn_bo",
        "L0_ffn_fast_b", "L0_ffn_w_fc", "L0_ffn_w_proj", "L0_ffn_u", "L0_ffn_v", "L0_ffn_gate"]


def kernel(**inputs):
    import numpy as _np
    import concourse.bacc as _bacc
    from concourse.bass_utils import run_bass_kernel_spmd as _run

    nc = _bacc.Bacc("TRN2", target_bir_lowering=False, num_devices=1)
    arrays, args = {}, []
    for name in _INS:
        a = _np.ascontiguousarray(inputs[name])
        if a.ndim == 0:
            a = a.reshape(1, 1)
        arrays[f"in_{name}_dram"] = a
        args.append(nc.dram_tensor(f"in_{name}_dram", a.shape, mybir.dt.from_np(a.dtype), kind="ExternalInput").ap())
    shape = inputs["x"].shape
    args.append(nc.dram_tensor("out_0_dram", shape, F32, kind="ExternalOutput").ap())
    xattn_ffn_kernel(nc, *args)
    r = _run(nc, [arrays], core_ids=[0])
    return r.results[0]["out_0_dram"]
```
